# Optimizing a Trainium2 kernel written in Bass

```python
import numpy as np
import jax
import jax.numpy as jnp

def _softmax(x, axis=-1):
    return jax.nn.softmax(x, axis=axis)

def _gelu(x):
    return jax.nn.gelu(x, approximate=True)

def _silu(x):
    return jax.nn.silu(x)

def _sigmoid(x):
    return jax.nn.sigmoid(x)

def _layernorm(x, axis=-1, eps=1e-05):
    m = jnp.mean(x, axis=axis, keepdims=True)
    v = jnp.var(x, axis=axis, keepdims=True)
    return (x - m) / jnp.sqrt(v + eps)

def _scatter_add(tgt, idx, src, axis=0):
    return tgt.at[idx].add(src)

def _segment_sum(src, seg, n):
    return jax.ops.segment_sum(src, seg, n)
kernel_name = 'mk_seq_postln_d1_jaxref_r4_eeb309'

def setup_inputs(seed: int=0):
    np.random.seed(seed)
    _w = jnp.asarray

    def _L0_attn_setup():
        import jax, jax.numpy as jnp
        import numpy as np
        D_MODEL = 256
        D_STATE = 16
        D_CONV = 4
        EXPAND = 2
        D_INNER = EXPAND * D_MODEL
        DT_RANK = D_MODEL // 16
        BATCH = 2
        SEQ = 512

        def _selective_scan(u, dt, A, Bm, Cm, D):

            def step(h, xs):
                u_t, dt_t, B_t, C_t = xs
                dA = jnp.exp(dt_t[:, :, None] * A)
                h = dA * h + (dt_t * u_t)[:, :, None] * B_t[:, None, :]
                y = jnp.einsum('bdn,bn->bd', h, C_t)
                return (h, y)
            xs = (u.transpose(1, 0, 2), dt.transpose(1, 0, 2), Bm.transpose(1, 0, 2), Cm.transpose(1, 0, 2))
            h0 = jnp.zeros((u.shape[0], u.shape[2], A.shape[1]), u.dtype)
            _, ys = jax.lax.scan(step, h0, xs)
            return ys.transpose(1, 0, 2) + u * D
        key = jax.random.key(seed)
        ks = jax.random.split(key, 8)
        s = 0.02
        x = jax.random.normal(ks[0], (BATCH, SEQ, D_MODEL), jnp.float32)
        in_proj_w = jax.random.normal(ks[1], (D_MODEL, 2 * D_INNER), jnp.float32) * s
        conv_w = jax.random.normal(ks[2], (D_INNER, 1, D_CONV), jnp.float32) * s
        conv_b = jnp.zeros((D_INNER,), jnp.float32)
        x_proj_w = jax.random.normal(ks[3], (D_INNER, DT_RANK + 2 * D_STATE), jnp.float32) * s
        dt_proj_w = jax.random.normal(ks[4], (DT_RANK, D_INNER), jnp.float32) * s
        dt_proj_b = jnp.full((D_INNER,), -4.6, jnp.float32)
        A_log = jnp.log(jnp.broadcast_to(jnp.arange(1, D_STATE + 1, dtype=jnp.float32), (D_INNER, D_STATE)))
        D = jnp.ones((D_INNER,), jnp.float32)
        out_proj_w = jax.random.normal(ks[5], (D_INNER, D_MODEL), jnp.float32) * s
        fg_w = jax.random.normal(ks[6], (D_MODEL, D_MODEL), jnp.float32) * s
        fg_b = jnp.zeros((D_MODEL,), jnp.float32)
        return dict(x=x, in_proj_w=in_proj_w, conv_w=conv_w, conv_b=conv_b, x_proj_w=x_proj_w, dt_proj_w=dt_proj_w, dt_proj_b=dt_proj_b, A_log=A_log, D=D, out_proj_w=out_proj_w, fg_w=fg_w, fg_b=fg_b)
    _L0_attn_in = _L0_attn_setup()

    def _L0_ffn_setup():
        import jax, jax.numpy as jnp
        import numpy as np
        DIM = 256
        HIDDEN = 768
        SCALE = 1.0 / 127.0

        def _dequant(w_int, dtype):
            return w_int.astype(dtype) * jnp.asarray(SCALE, dtype)
        key = jax.random.key(seed)
        k_x, k_g, k_u, k_d = jax.random.split(key, 4)
        x = jax.random.normal(k_x, (4, 512, DIM), dtype=jnp.float32)
        w_gate = jax.random.randint(k_g, (HIDDEN, DIM), -127, 128, dtype=jnp.int32)
        w_up = jax.random.randint(k_u, (HIDDEN, DIM), -127, 128, dtype=jnp.int32)
        w_down = jax.random.randint(k_d, (DIM, HIDDEN), -127, 128, dtype=jnp.int32)
        return {'x': x, 'w_gate': w_gate, 'w_up': w_up, 'w_down': w_down}
    _L0_ffn_in = _L0_ffn_setup()
    _d = {'L0_attn_x': _L0_attn_in['x'], 'L0_attn_in_proj_w': _L0_attn_in['in_proj_w'], 'L0_attn_conv_w': _L0_attn_in['conv_w'], 'L0_attn_conv_b': _L0_attn_in['conv_b'], 'L0_attn_x_proj_w': _L0_attn_in['x_proj_w'], 'L0_attn_dt_proj_w': _L0_attn_in['dt_proj_w'], 'L0_attn_dt_proj_b': _L0_attn_in['dt_proj_b'], 'L0_attn_A_log': _L0_attn_in['A_log'], 'L0_attn_D': _L0_attn_in['D'], 'L0_attn_out_proj_w': _L0_attn_in['out_proj_w'], 'L0_attn_fg_w': _L0_attn_in['fg_w'], 'L0_attn_fg_b': _L0_attn_in['fg_b'], 'L0_ffn_w_gate': _L0_ffn_in['w_gate'], 'L0_ffn_w_up': _L0_ffn_in['w_up'], 'L0_ffn_w_down': _L0_ffn_in['w_down']}
    _x0 = _d['L0_attn_x']
    _d['L0_attn_x'] = jax.random.normal(jax.random.fold_in(jax.random.key(seed), 1), (8, 512, 256), dtype=_x0.dtype)
    del _x0
    return _d

def reference(L0_attn_x, L0_attn_in_proj_w, L0_attn_conv_w, L0_attn_conv_b, L0_attn_x_proj_w, L0_attn_dt_proj_w, L0_attn_dt_proj_b, L0_attn_A_log, L0_attn_D, L0_attn_out_proj_w, L0_attn_fg_w, L0_attn_fg_b, L0_ffn_w_gate, L0_ffn_w_up, L0_ffn_w_down):

    def _L0_attn_ref(x, in_proj_w, conv_w, conv_b, x_proj_w, dt_proj_w, dt_proj_b, A_log, D, out_proj_w, fg_w, fg_b):
        import jax, jax.numpy as jnp
        import numpy as np
        D_MODEL = 256
        D_STATE = 16
        D_CONV = 4
        EXPAND = 2
        D_INNER = EXPAND * D_MODEL
        DT_RANK = D_MODEL // 16
        BATCH = 2
        SEQ = 512

        def _selective_scan(u, dt, A, Bm, Cm, D):

            def step(h, xs):
                u_t, dt_t, B_t, C_t = xs
                dA = jnp.exp(dt_t[:, :, None] * A)
                h = dA * h + (dt_t * u_t)[:, :, None] * B_t[:, None, :]
                y = jnp.einsum('bdn,bn->bd', h, C_t)
                return (h, y)
            xs = (u.transpose(1, 0, 2), dt.transpose(1, 0, 2), Bm.transpose(1, 0, 2), Cm.transpose(1, 0, 2))
            h0 = jnp.zeros((u.shape[0], u.shape[2], A.shape[1]), u.dtype)
            _, ys = jax.lax.scan(step, h0, xs)
            return ys.transpose(1, 0, 2) + u * D
        silu = jax.nn.silu
        xz = x @ in_proj_w
        xi, z = jnp.split(xz, 2, axis=-1)
        xt = xi.transpose(0, 2, 1)
        conv = jax.lax.conv_general_dilated(xt, conv_w, (1,), [(D_CONV - 1, 0)], dimension_numbers=('NCH', 'OIH', 'NCH'), feature_group_count=D_INNER)
        xi = silu((conv + conv_b[None, :, None]).transpose(0, 2, 1))
        x_dbl = xi @ x_proj_w
        dt = x_dbl[..., :DT_RANK]
        Bm = x_dbl[..., DT_RANK:DT_RANK + D_STATE]
        Cm = x_dbl[..., DT_RANK + D_STATE:]
        dt = jax.nn.softplus(dt @ dt_proj_w + dt_proj_b)
        A = -jnp.exp(A_log)
        y = _selective_scan(xi, dt, A, Bm, Cm, D)
        y = y * silu(z)
        new_features = y @ out_proj_w
        fg = jax.nn.sigmoid(x @ fg_w + fg_b)
        return fg * x + (1.0 - fg) * new_features

    def _L0_ffn_ref(x, w_gate, w_up, w_down):
        import jax, jax.numpy as jnp
        import numpy as np
        DIM = 256
        HIDDEN = 768
        SCALE = 1.0 / 127.0

        def _dequant(w_int, dtype):
            return w_int.astype(dtype) * jnp.asarray(SCALE, dtype)
        wg = _dequant(w_gate, x.dtype)
        wu = _dequant(w_up, x.dtype)
        wd = _dequant(w_down, x.dtype)
        gate = jnp.einsum('bsd,hd->bsh', x, wg)
        up = jnp.einsum('bsd,hd->bsh', x, wu)
        h = jax.nn.silu(gate) * up
        return jnp.einsum('bsh,dh->bsd', h, wd)
    x = L0_attn_x
    x = _layernorm(x + _L0_attn_ref(x, L0_attn_in_proj_w, L0_attn_conv_w, L0_attn_conv_b, L0_attn_x_proj_w, L0_attn_dt_proj_w, L0_attn_dt_proj_b, L0_attn_A_log, L0_attn_D, L0_attn_out_proj_w, L0_attn_fg_w, L0_attn_fg_b), axis=-1)
    x = _layernorm(x + _L0_ffn_ref(x, L0_ffn_w_gate, L0_ffn_w_up, L0_ffn_w_down), axis=-1)
    return x

_drawn_inputs = setup_inputs


def setup_inputs(seed=0):
    import zlib

    import numpy as np

    out = dict(_drawn_inputs(seed))
    spreads = {'L0_attn_conv_b': (0.0, 0.8),
     'L0_attn_dt_proj_b': (-4.599999904632568, 0.6),
     'L0_attn_D': (1.0, 0.6),
     'L0_attn_fg_b': (0.0, 0.341)}
    factors = {'L0_attn_in_proj_w': 8.0,
     'L0_attn_conv_w': 8.0,
     'L0_attn_x_proj_w': 8.0,
     'L0_attn_dt_proj_w': 8.0,
     'L0_attn_A_log': 8.0,
     'L0_attn_out_proj_w': 8.0}
    for name, (base, spread) in spreads.items():
        noise = np.random.default_rng([zlib.crc32(name.encode()), seed]).standard_normal(out[name].shape)
        drawn = base * np.exp(spread * noise) if base else spread * noise
        out[name] = jnp.asarray(drawn.astype(out[name].dtype))
    for name, factor in factors.items():
        out[name] = (out[name] * factor).astype(out[name].dtype)
    return out
```

```python
from contextlib import ExitStack

import concourse.bass as bass
from concourse import mybir

F32 = mybir.dt.float32
BF16 = mybir.dt.bfloat16
I32 = mybir.dt.int32
ALU = mybir.AluOpType
ACT = mybir.ActivationFunctionType

BATCH, SEQ, DM = 8, 512, 256
DI, NS, TAPS, RANK = 512, 16, 4, 16
HID = 768
P = 128
NK = DI // P
KM = DM // P
TB = SEQ // P
NC = HID // P
UNITS = NK * NS
EPS = 1e-5
DEQUANT = 1.0 / 127.0

POOL_N = (2, 7, 12)
VEC_N = [n for n in range(NS) if n not in POOL_N]
DBU_RING, PROD_RING = 4, 3
ONE = 1
BC_PARTS = 96
DT_ROW = 96

TRIPS = (BATCH - 2) // 2

class Batch:

    def __init__(self, const, trip=None):
        self.const, self.trip = const, trip

    def __add__(self, d):
        return Batch(self.const + d, self.trip)

    def __sub__(self, d):
        return Batch(self.const - d, self.trip)

    @property
    def parity(self):
        return self.const % 2

    def times(self, per, extra=0):
        if self.trip is None:
            return per * self.const + extra
        return self.trip * (2 * per) + (per * self.const + extra)


def reach(eng, sem, b, per, extra):
    if per * b.const + extra <= 0:
        assert b.trip is None
        return
    eng.wait_ge(sem, b.times(per, extra))


def batches(eng, iteration):
    for c in (-1, 0):
        iteration(Batch(c))
    with eng.Fori(0, TRIPS) as trip:
        for c in (1, 2):
            iteration(Batch(c, trip))
    for c in (BATCH - 1, BATCH):
        iteration(Batch(c))


def has_post(b):
    return b.trip is not None or b.const >= 1


def has_scan(b):
    return b.trip is not None or 0 <= b.const < BATCH


def has_pre(b):
    return b.trip is not None or b.const < BATCH - 1


def build(nc, x, xT, in_w, conv_w, conv_b, xp_w, dt_w, dt_b, a_log, d_skip, out_w, fg_w, fg_b,
          gate_wT, up_wT, down_wT, ident, eye3, out):
    ctx = ExitStack()
    with ctx:
        def sb(name, shape, dt=F32):
            return ctx.enter_context(nc.sbuf_tensor(name, shape, dt))

        def ps(name):
            return ctx.enter_context(nc.psum_tensor(name, [P, SEQ], F32))

        def sem(name):
            return ctx.enter_context(nc.semaphore(name))

        Win = sb("Win", [P, KM, 2 * DI])
        Wxp = sb("Wxp", [P, NK, BC_PARTS + RANK])
        Wout = sb("Wout", [P, NK, DM])
        Wfg = sb("Wfg", [P, KM, DM])
        FgB = sb("FgB", [1, DM])
        Wgate = sb("Wgate", [P, KM, HID])
        Wup = sb("Wup", [P, KM, HID])
        Wdown = sb("Wdown", [P, NC, DM])
        Id = sb("Id", [P, P])
        Eye3 = sb("Eye3", [BC_PARTS, 2 * NS])
        SelDt = sb("SelDt", [P, 2 * NS, P], BF16)
        Sel = SelDt[0:BC_PARTS, :, :]
        Wdt = SelDt[:, 0:2 * DI // P, :].rearrange("p r c -> p (r c)").bitcast(F32)
        DiagD = sb("DiagD", [P, NK, P])
        ConvW = sb("ConvW", [P, NK, TAPS])
        ConvB = sb("ConvB", [P, NK])
        Dcol = sb("Dcol", [P, NK])
        NegA = sb("NegA", [P, NK, NS])
        Ones = sb("Ones", [1, P])
        MinusHalf = sb("MinusHalf", [P, TB])
        Eps = sb("Eps", [P, 2, TB])

        XT = sb("XT", [P, 2, KM, SEQ])
        XN = sb("XN", [P, TB, DM])
        Bc = sb("Bc", [P, NS, SEQ])
        Cc = sb("Cc", [P, NS, SEQ])
        Xi = sb("Xi", [P, TAPS - 1 + SEQ])
        U = sb("U", [P, 2, NK, SEQ])
        TanhC = sb("TanhC", [P, SEQ])
        DblS = sb("DblS", [BC_PARTS, SEQ], BF16)
        Dbl = sb("Dbl", [P, SEQ])
        Sp_e = sb("Sp_e", [P, SEQ])
        Sp_ln = sb("Sp_ln", [P, SEQ])
        Sp_fix = sb("Sp_fix", [P, SEQ])
        Sp_relu = sb("Sp_relu", [P, SEQ])
        Dt = sb("Dt", [P, 2, SEQ])
        DtU = sb("DtU", [P, 2, SEQ])
        DBu = sb("DBu", [P, DBU_RING, SEQ])
        Prod = sb("Prod", [P, PROD_RING, SEQ])
        Hs = sb("Hs", [P, SEQ])
        G = sb("G", [P, TB, P])
        Gt = sb("Gt", [P, NK, SEQ])
        TanhF = sb("TanhF", [P, TB, DM])
        X1 = sb("X1", [P, TB, DM])
        Ht = sb("Ht", [P, NC, SEQ])
        Stats1 = sb("Stats1", [P, TB, 6])
        Mv1 = sb("Mv1", [P, TB, 2])
        Rs1 = sb("Rs1", [P, TB])
        Stats2 = sb("Stats2", [P, TB, 6])
        Mv2 = sb("Mv2", [P, TB, 2])
        Rs2 = sb("Rs2", [P, TB])
        X1t = Gt[:, 2:4, :]

        dA = [ps(f"dA{i}") for i in range(2)]
        H = [ps(f"H{i}") for i in range(2)]
        Y = ps("Y")
        W = {name: ps(f"work{name}") for name in "ABC"}

        w_loaded = sem("w_loaded")
        xt_loaded = [sem(f"xt_loaded{i}") for i in range(2)]
        xn_loaded = sem("xn_loaded")
        stored = sem("stored")
        w_ready = sem("w_ready")
        a_ready = sem("a_ready")
        sel_ready = sem("sel_ready")
        xi_done = sem("xi_done")
        xi_copied = sem("xi_copied")
        tap_done = sem("tap_done")
        tanh_c = sem("tanh_c")
        u_ready = sem("u_ready")
        dbl_done = sem("dbl_done")
        split_hi = sem("split_hi")
        rest1 = sem("rest1")
        split_mid = sem("split_mid")
        rest2 = sem("rest2")
        split_lo = sem("split_lo")
        bcB_done, bcC_done = sem("bcB_done"), sem("bcC_done")
        B_ready, C_ready = sem("B_ready"), sem("C_ready")
        v_done = sem("v_done")
        sp_abs = sem("sp_abs")
        sp_e = sem("sp_e")
        sp_ln = sem("sp_ln")
        sp_rounded = sem("sp_rounded")
        sp_lost = sem("sp_lost")
        sp_sum = sem("sp_sum")
        dt_ready = sem("dt_ready")
        dtu_ready = sem("dtu_ready")
        dA_ready = sem("dA_ready")
        dBu_ready = sem("dBu_ready")
        h_ready = sem("h_ready")
        prod_vec = sem("prod_vec")
        prod_pool = sem("prod_pool")
        y_added = sem("y_added")
        z_done = sem("z_done")
        tanh_z = sem("tanh_z")
        silu_z = sem("silu_z")
        g_ready = sem("g_ready")
        gt_done = sem("gt_done")
        gt_copied = sem("gt_copied")
        fg_done = sem("fg_done")
        tanh_f = sem("tanh_f")
        nf_done = sem("nf_done")
        mix_parts = sem("mix_parts")
        mixed = sem("mixed")
        stats1 = sem("stats1")
        mv1 = sem("mv1")
        var1 = sem("var1")
        rs1 = sem("rs1")
        x1_ready = sem("x1_ready")
        x1t_done = sem("x1t_done")
        x1t_copied = sem("x1t_copied")
        gate_done, up_done = sem("gate_done"), sem("up_done")
        tanh_g = sem("tanh_g")
        silu_g = sem("silu_g")
        hid_ready = sem("hid_ready")
        down_done = sem("down_done")
        summed = sem("summed")
        stats2 = sem("stats2")
        mv2 = sem("mv2")
        var2 = sem("var2")
        rs2 = sem("rs2")
        out_ready = sem("out_ready")

        gate_stage = Bc[:, 0:3, :].rearrange("p a b -> p (a b)").bitcast(I32)
        up_stage = Bc[:, 3:6, :].rearrange("p a b -> p (a b)").bitcast(I32)
        down_stage = Bc[:, 6:9, :].rearrange("p a b -> p (a b)").bitcast(I32)

        block = ctx.enter_context(nc.Block())

        @block.sync
        def _(sp):
            def rows(dram, b, count):
                if b.trip is None:
                    return dram[b.times(count):b.times(count) + count, :]
                return dram[bass.ds(sp.snap(b.times(count)), count), :]

            loads = [
                (Win[:, :, :], in_w.rearrange("(k p) n -> p k n", p=P)),
                (ConvW[:, :, :], conv_w.rearrange("(k p) o t -> p k (o t)", p=P)),
                (ConvB[:, :], conv_b),
                (Wxp[:, :, 0:32], xp_w[:, RANK:RANK + 2 * NS].rearrange("(k p) n -> p k n", p=P)),
                (Wxp[:, :, 32:64], xp_w[:, RANK:RANK + 2 * NS].rearrange("(k p) n -> p k n", p=P)),
                (Wxp[:, :, 64:96], xp_w[:, RANK:RANK + 2 * NS].rearrange("(k p) n -> p k n", p=P)),
                (Wxp[:, :, 96:96 + RANK], xp_w[:, 0:RANK].rearrange("(k p) n -> p k n", p=P)),
                (Wdt[DT_ROW:DT_ROW + RANK, :], dt_w),
                (Wdt[DT_ROW + RANK:DT_ROW + RANK + 1, :], dt_b.rearrange("(o n) -> o n", o=1)),
                (NegA[:, :, :], a_log.rearrange("(k p) n -> p k n", p=P)),
                (Dcol[:, :], d_skip),
                (Id[:, :], ident),
                (Eye3[:, :], eye3),
                (Wout[:, :, :], out_w.rearrange("(k p) n -> p k n", p=P)),
                (Wfg[:, :, :], fg_w.rearrange("(k p) n -> p k n", p=P)),
                (FgB[:, :], fg_b.rearrange("(o n) -> o n", o=1)),
                (gate_stage.rearrange("p (k n) -> p k n", k=KM), gate_wT.rearrange("(k p) n -> p k n", p=P)),
                (up_stage.rearrange("p (k n) -> p k n", k=KM), up_wT.rearrange("(k p) n -> p k n", p=P)),
                (down_stage.rearrange("p (k n) -> p k n", k=NC), down_wT.rearrange("(k p) n -> p k n", p=P)),
            ]
            assert len(loads) == LOADS
            def load_xt(b, source):
                sp.dma_start(XT[:, b.parity, :, :], source.rearrange("(k p) t -> p k t", p=P)
                             ).then_inc(xt_loaded[b.parity], 16)

            load_xt(Batch(0), rows(xT, Batch(0), KM * P))
            for dst, src in loads:
                sp.dma_start(dst, src).then_inc(w_loaded, 16)

            def iteration(b):
                if has_scan(b) and has_pre(b):
                    source = rows(xT, b + 1, KM * P)
                    reach(sp, z_done, b - 1, NK, NK)
                    load_xt(b + 1, source)
                if has_scan(b):
                    source = rows(x, b, SEQ)
                    reach(sp, mixed, b - 1, 2, 2)
                    sp.dma_start(XN[:, :, :], source.rearrange("(t p) d -> p t d", p=P)).then_inc(xn_loaded, 16)
                if has_post(b):
                    target = rows(out, b - 1, SEQ)
                    reach(sp, out_ready, b - 1, 1, 1)
                    sp.dma_start(target.rearrange("(t p) d -> p t d", p=P), X1[:, :, :]).then_inc(stored, 16)

            batches(sp, iteration)
            sp.wait_ge(stored, 16 * BATCH + ONE)

        @block.tensor
        def _(pe):
            read_by = {name: None for name in W}

            def take(name, sem, b, per, extra):
                if read_by[name]:
                    before, when, *count = read_by[name]
                    pe.wait_ge(before, when.times(*count))
                read_by[name] = (sem, b, per, extra)
                return W[name]

            def xi(b, j):
                if j == 0:
                    before = 16 * (b.const // 2)
                    pe.wait_ge(xt_loaded[b.parity], before + 16 if b.trip is None else b.trip * 16 + (before + 16))
                bank = take("B" if j == 1 else "A", xi_copied, b, NK, j + 1)
                for k in range(KM):
                    mm = nc.tensor.matmul(bank[:, :], Win[:, k, j * P:(j + 1) * P], XT[:, b.parity, k, :],
                                          start=(k == 0), stop=(k == KM - 1))
                mm.then_inc(xi_done, 1)

            def x_proj(b):
                bank = take("C", rest1, b, 1, 1)
                reach(pe, u_ready, b, NK, NK)
                for k in range(NK):
                    mm = nc.tensor.matmul(bank[0:BC_PARTS + RANK, :], Wxp[:, k, :], U[:, b.parity, k, :],
                                          start=(k == 0), stop=(k == NK - 1))
                mm.then_inc(dbl_done, 1)

            def broadcast(b, n):
                if n == 0:
                    reach(pe, split_lo, b, 1, 1)
                for name, row, done, ready in (("A", n, bcB_done, B_ready), ("B", NS + n, bcC_done, C_ready)):
                    bank = take(name, ready, b, NS, n + 1)
                    nc.tensor.matmul(bank[:, :], Sel[:, row, :], DblS[:, :], start=True, stop=True).then_inc(done, 1)

            def dt_arg(b, k):
                bank = take("C", sp_abs, b, NK, k + 1)
                if k == 0:
                    reach(pe, split_hi, b, 1, 1)
                rows = slice(DT_ROW, DT_ROW + RANK + 1)
                nc.tensor.matmul(bank[:, :], Wdt[rows, k * P:(k + 1) * P], Dbl[rows, :],
                                 start=True, stop=True).then_inc(v_done, 1)

            def z(b, k):
                bank = take("C", silu_z, b, NK, k + 1)
                for t in range(TB):
                    for c in range(KM):
                        mm = nc.tensor.matmul(bank[:, t * P:(t + 1) * P], XT[:, b.parity, c, t * P:(t + 1) * P],
                                              Win[:, c, DI + k * P:DI + (k + 1) * P],
                                              start=(c == 0), stop=(c == KM - 1))
                mm.then_inc(z_done, 1)

            def feature_gate(b, half):
                bank = take("C", tanh_f, b, 2, half + 1)
                for t in range(2):
                    rows = slice((2 * half + t) * P, (2 * half + t + 1) * P)
                    for c in range(KM):
                        nc.tensor.matmul(bank[:, t * DM:(t + 1) * DM], XT[:, b.parity, c, rows], Wfg[:, c, :],
                                         start=(c == 0), stop=False)
                    mm = nc.tensor.matmul(bank[:, t * DM:(t + 1) * DM], Ones[:, :], FgB[:, :], start=False, stop=True)
                mm.then_inc(fg_done, 1)

            def y_skip(b, k):
                if k or has_post(b):
                    reach(pe, g_ready, b, NK, k)
                for t in range(TB):
                    nc.tensor.matmul(Y[:, t * P:(t + 1) * P], U[:, b.parity, k, t * P:(t + 1) * P], DiagD[:, k, :],
                                     start=(t == 0), stop=False, skip_group_check=True)

            def y_add(b, k, n):
                unit = k * NS + n
                if n in POOL_N:
                    reach(pe, prod_pool, b, NK * len(POOL_N), k * len(POOL_N) + POOL_N.index(n) + 1)
                else:
                    reach(pe, prod_vec, b, NK * len(VEC_N), k * len(VEC_N) + VEC_N.index(n) + 1)
                slot = unit % PROD_RING
                for t in range(TB):
                    mm = nc.tensor.matmul(Y[:, t * P:(t + 1) * P], Prod[:, slot, t * P:(t + 1) * P], Id[:, :],
                                          start=False, stop=(n == NS - 1), is_transpose=True,
                                          skip_group_check=True)
                mm.then_inc(y_added, 1)

            def g_transpose(b, k):
                bank = take("C", gt_copied, b, NK, k + 1)
                reach(pe, g_ready, b, NK, k + 1)
                for t in range(TB):
                    mm = nc.tensor.transpose(bank[:, t * P:(t + 1) * P], G[:, t, :], Id[:, :])
                mm.then_inc(gt_done, 1)

            def out_proj(b, t):
                if t == 0:
                    reach(pe, gt_copied, b, NK, NK)
                if t % 2 == 0:
                    take("A", mix_parts, b, 4, t + 2)
                for c in range(NK):
                    mm = nc.tensor.matmul(W["A"][:, (t % 2) * DM:(t % 2 + 1) * DM], Gt[:, c, t * P:(t + 1) * P],
                                          Wout[:, c, :], start=(c == 0), stop=(c == NK - 1))
                if t % 2:
                    mm.then_inc(nf_done, 1)

            def x1_transpose(b, c):
                bank = take("B", x1t_copied, b, KM, c + 1)
                if c == 0:
                    reach(pe, x1_ready, b, 1, 1)
                for t in range(TB):
                    mm = nc.tensor.transpose(bank[:, t * P:(t + 1) * P], X1[:, t, c * P:(c + 1) * P], Id[:, :])
                mm.then_inc(x1t_done, 1)

            def hidden(b, c, name, weights, done, read):
                bank = take(name, read, b, NC, c + 1)
                if c == 0:
                    reach(pe, x1t_copied, b, KM, KM)
                for k in range(KM):
                    mm = nc.tensor.matmul(bank[:, :], weights[:, k, c * P:(c + 1) * P], X1t[:, k, :],
                                          start=(k == 0), stop=(k == KM - 1))
                mm.then_inc(done, 1)

            def down(b, t):
                if t == 0:
                    reach(pe, hid_ready, b, NC, NC)
                if t % 2 == 0:
                    take("C", summed, b, 2, t // 2 + 1)
                for c in range(NC):
                    mm = nc.tensor.matmul(W["C"][:, (t % 2) * DM:(t % 2 + 1) * DM], Ht[:, c, t * P:(t + 1) * P],
                                          Wdown[:, c, :], start=(c == 0), stop=(c == NC - 1))
                if t % 2:
                    mm.then_inc(down_done, 1)

            def iteration(b):
                post, scan, pre = has_post(b), has_scan(b), has_pre(b)
                for s in range(UNITS):
                    k, n = divmod(s, NS)
                    if scan:
                        if n == 0:
                            y_skip(b, k)
                        y_add(b, k, n)
                        if s < 2:
                            broadcast(b, NS - 2 + s)
                    if s == 2 and post:
                        g_transpose(b - 1, NK - 1)
                    if n == 2 and k and scan:
                        g_transpose(b, k - 1)
                    if n == 3 and k < NK - 1 and scan:
                        dt_arg(b, k + 1)
                    if s == 51 and pre:
                        dt_arg(b + 1, 0)
                    if n == 10 and scan:
                        z(b, k)
                    if s in (5, 6, 7, 8) and post:
                        out_proj(b - 1, s - 5)
                    if s in XI_SLOTS and pre:
                        xi(b + 1, XI_SLOTS.index(s))
                    if s in (17, 18) and post:
                        x1_transpose(b - 1, s - 17)
                    if s in GATE_SLOTS and post:
                        hidden(b - 1, GATE_SLOTS.index(s), "A", Wgate, gate_done, silu_g)
                    if s - 2 in GATE_SLOTS and post:
                        hidden(b - 1, GATE_SLOTS.index(s - 2), "B", Wup, up_done, hid_ready)
                    if s == 37 and pre:
                        x_proj(b + 1)
                    if s in (46, 48) and scan:
                        feature_gate(b, (s - 46) // 2)
                    if s in DOWN_SLOTS and post:
                        down(b - 1, DOWN_SLOTS.index(s))
                    if s >= 50 and pre:
                        broadcast(b + 1, s - 50)

            pe.wait_ge(w_loaded, 16 * LOADS)
            pe.wait_ge(w_ready, 1)
            for c in (-1, 0):
                iteration(Batch(c))
            with pe.Fori(0, TRIPS) as trip:
                for name, (sem_, b, *count) in read_by.items():
                    read_by[name] = (sem_, Batch(b.const, trip), *count)
                for c in (1, 2):
                    iteration(Batch(c, trip))
            for name, (sem_, b, *count) in read_by.items():
                read_by[name] = (sem_, Batch(b.const + 2 * (TRIPS - 1)), *count)
            for c in (BATCH - 1, BATCH):
                iteration(Batch(c))

        @block.scalar
        def _(act):
            def xi_copy(b, j):
                reach(act, xi_done, b, NK, j + 1)
                reach(act, tap_done, b, NK * (TAPS - 1), j * (TAPS - 1))
                reach(act, y_added, b - 2, UNITS, UNITS)
                reach(act, dtu_ready, b - 2, NK, NK)
                bank = W["B" if j == 1 else "A"]
                nc.scalar.activation(Xi[:, TAPS - 1:], bank[:, :], ACT.Copy)
                nc.scalar.activation(U[:, b.parity, j, :], bank[:, :], ACT.Identity, bias=ConvB[:, j:j + 1],
                                     scale=ConvW[:, j, TAPS - 1:TAPS]).then_inc(xi_copied, 1)

            def xi_tanh(b, j):
                reach(act, tap_done, b, NK * (TAPS - 1), (j + 1) * (TAPS - 1))
                reach(act, u_ready, b, NK, j)
                nc.scalar.activation(TanhC[:, :], U[:, b.parity, j, :], ACT.Tanh).then_inc(tanh_c, 1)

            def split(b, part):
                if part == 0:
                    reach(act, dbl_done, b, 1, 1)
                    reach(act, bcC_done, b, NS, 0)
                    reach(act, v_done, b, NK, 0)
                    reach(act, split_lo, b, 1, 0)
                    rows = slice(DT_ROW, DT_ROW + RANK)
                    nc.scalar.activation(Dbl[rows, :], W["C"][rows, :], ACT.Copy)
                    nc.scalar.activation(DblS[:, :], W["C"][0:BC_PARTS, :], ACT.Copy).then_inc(split_hi, 1)
                elif part == 1:
                    reach(act, rest1, b, 1, 1)
                    nc.scalar.activation(DblS[32:64, :], Dbl[32:64, :], ACT.Copy)
                    nc.scalar.activation(DblS[64:96, :], Dbl[64:96, :], ACT.Copy).then_inc(split_mid, 1)
                else:
                    reach(act, rest2, b, 1, 1)
                    nc.scalar.activation(DblS[64:96, :], Dbl[64:96, :], ACT.Copy).then_inc(split_lo, 1)

            def bc_copy(b, n):
                last = NK - 1
                reach(act, bcB_done, b, NS, n + 1)
                reach(act, dBu_ready, b - 1, UNITS, last * NS + n + 1)
                nc.scalar.activation(Bc[:, n, :], W["A"][:, :], ACT.Copy).then_inc(B_ready, 1)
                reach(act, bcC_done, b, NS, n + 1)
                if n in POOL_N:
                    reach(act, prod_pool, b - 1, NK * len(POOL_N), last * len(POOL_N) + POOL_N.index(n) + 1)
                else:
                    reach(act, prod_vec, b - 1, NK * len(VEC_N), last * len(VEC_N) + VEC_N.index(n) + 1)
                nc.scalar.activation(Cc[:, n, :], W["B"][:, :], ACT.Copy).then_inc(C_ready, 1)

            def softplus(b, k):
                m = k + 1
                reach(act, v_done, b, NK, m)
                reach(act, dt_ready, b, NK, m - 1)
                nc.scalar.activation(Sp_relu[:, :], W["C"][:, :], ACT.Relu)
                reach(act, sp_lost, b, NK, m - 1)
                reach(act, sp_ln, b, NK, m - 1)
                nc.scalar.activation(Sp_e[:, :], W["C"][:, :], ACT.Abs).then_inc(sp_abs, 1)
                act.wait_ge(sp_abs, b.times(NK, m))
                nc.scalar.activation(Sp_e[:, :], Sp_e[:, :], ACT.Exp, scale=-1.0).then_inc(sp_e, 1)

            def softplus_ln(b, k):
                act.wait_ge(sp_e, b.times(NK, k + 1))
                reach(act, sp_sum, b, NK, k)
                nc.scalar.activation(Sp_ln[:, :], Sp_e[:, :], ACT.Ln, bias=1.0).then_inc(sp_ln, 1)

            def decay(b, k, n):
                unit = k * NS + n
                if n == 0:
                    reach(act, dt_ready, b, NK, k + 1)
                reach(act, h_ready, b, UNITS, unit - 1)
                nc.scalar.activation(dA[unit % 2][:, :], Dt[:, k % 2, :], ACT.Exp,
                                     scale=NegA[:, k, n:n + 1]).then_inc(dA_ready, 1)

            def z_tanh(b, k):
                reach(act, z_done, b, NK, k + 1)
                reach(act, gt_done, b, NK, k)
                nc.scalar.activation(G[:, :, :].rearrange("p t d -> p (t d)"), W["C"][:, :], ACT.Tanh,
                                     scale=0.5).then_inc(tanh_z, 1)

            def gt_copy(b, k):
                reach(act, gt_done, b, NK, k + 1)
                if k < 2:
                    reach(act, nf_done, b, 2, 0)
                else:
                    reach(act, up_done, b, NC, ONE)
                    reach(act, gate_done, b, NC, ONE)
                nc.scalar.activation(Gt[:, k, :], W["C"][:, :], ACT.Copy, scale=0.5).then_inc(gt_copied, 1)

            def fg_tanh(b, half):
                reach(act, fg_done, b, 2, half + 1)
                reach(act, mixed, b, 2, 0)
                nc.scalar.activation(TanhF[:, 2 * half:2 * half + 2, :].rearrange("p t d -> p (t d)"),
                                     W["C"][:, :], ACT.Tanh, scale=0.5).then_inc(tanh_f, 1)

            def x1t_copy(b, c):
                reach(act, x1t_done, b, KM, c + 1)
                reach(act, nf_done, b, 2, 2)
                nc.scalar.activation(X1t[:, c, :], W["B"][:, :], ACT.Copy).then_inc(x1t_copied, 1)

            def gate_tanh(b, c):
                reach(act, gate_done, b, NC, ONE + c + 1)
                reach(act, down_done, b, 2, ONE)
                nc.scalar.activation(Ht[:, c, :], W["A"][:, :], ACT.Tanh, scale=0.5).then_inc(tanh_g, 1)

            def iteration(b):
                post, scan, pre = has_post(b), has_scan(b), has_pre(b)
                for s in range(UNITS):
                    k, n = divmod(s, NS)
                    if scan:
                        decay(b, k, n)
                        if s < 6:
                            bc_copy(b, NS - 6 + s)
                    if s == 7 and post:
                        gt_copy(b - 1, NK - 1)
                    if n == 7 and k and scan:
                        gt_copy(b, k - 1)
                    if n == 8 and k < NK - 1 and scan:
                        softplus(b, k + 1)
                    if n == 10 and k < NK - 1 and scan:
                        softplus_ln(b, k + 1)
                    if s == 56 and pre:
                        softplus(b + 1, 0)
                    if s == 58 and pre:
                        softplus_ln(b + 1, 0)
                    if n == 15 and scan:
                        z_tanh(b, k)
                    if s - 5 in XI_SLOTS and pre:
                        xi_copy(b + 1, XI_SLOTS.index(s - 5))
                    if s - 8 in XI_SLOTS and pre:
                        xi_tanh(b + 1, XI_SLOTS.index(s - 8))
                    if s in (22, 23) and post:
                        x1t_copy(b - 1, s - 22)
                    if s - 5 in GATE_SLOTS and post:
                        gate_tanh(b - 1, GATE_SLOTS.index(s - 5))
                    if s in (42, 44, 46) and pre:
                        split(b + 1, (s - 42) // 2)
                    if s in (51, 53) and scan:
                        fg_tanh(b, (s - 51) // 2)
                    if s >= 54 and pre:
                        bc_copy(b + 1, s - 54)

            act.wait_ge(w_loaded, 16 * LOADS)
            nc.scalar.activation(NegA[:, :, :], NegA[:, :, :], ACT.Exp).then_inc(a_ready, 1)
            act.wait_ge(w_ready, 1)
            batches(act, iteration)

        @block.gpsimd
        def _(pool):
            def lost(b, k):
                reach(pool, sp_rounded, b, NK, k + 1)
                nc.gpsimd.tensor_tensor(Sp_fix[:, :], Sp_e[:, :], Sp_fix[:, :], ALU.subtract).then_inc(sp_lost, 1)

            def log1p(b, k):
                reach(pool, sp_ln, b, NK, k + 1)
                pool.wait_ge(sp_lost, b.times(NK, k + 1))
                nc.gpsimd.tensor_tensor(Sp_fix[:, :], Sp_fix[:, :], Sp_ln[:, :], ALU.add).then_inc(sp_sum, 1)

            def dt_u(b, k):
                reach(pool, dt_ready, b, NK, k + 1)
                reach(pool, u_ready, b, NK, NK)
                reach(pool, dBu_ready, b, UNITS, (k - 1) * NS)
                nc.gpsimd.tensor_tensor(DtU[:, k % 2, :], Dt[:, k % 2, :], U[:, b.parity, k, :],
                                        ALU.mult).then_inc(dtu_ready, 1)

            def drive(b, k, n):
                unit = k * NS + n
                if k == 0:
                    reach(pool, B_ready, b, NS, n + 1)
                if n == 0:
                    pool.wait_ge(dtu_ready, b.times(NK, k + 1))
                reach(pool, h_ready, b, UNITS, unit + 1 - DBU_RING)
                nc.gpsimd.tensor_tensor(DBu[:, unit % DBU_RING, :], DtU[:, k % 2, :], Bc[:, n, :],
                                        ALU.mult).then_inc(dBu_ready, 1)

            def product(b, k, n):
                unit = k * NS + n
                reach(pool, h_ready, b, UNITS, unit + 1)
                if k == 0:
                    reach(pool, C_ready, b, NS, n + 1)
                reach(pool, y_added, b, UNITS, prod_slot_free(unit))
                nc.gpsimd.tensor_tensor(Prod[:, unit % PROD_RING, :], Hs[:, :], Cc[:, n, :],
                                        ALU.mult).then_inc(prod_pool, 1)

            def inverse_std(b, mv, Mv, var, Rs, rs, eps):
                reach(pool, mv, b, TB, TB)
                nc.gpsimd.tensor_tensor(Rs[:, :], Mv[:, :, 1], Eps[:, eps, :], ALU.add).then_inc(var, 1)
                pool.wait_ge(var, b.times(1, 1))
                nc.gpsimd.tensor_tensor(Rs[:, :], Rs[:, :], MinusHalf[:, :], ALU.pow).then_inc(rs, 1)

            def iteration(b):
                post, scan, pre = has_post(b), has_scan(b), has_pre(b)
                for s in range(UNITS):
                    k, n = divmod(s, NS)
                    if scan:
                        drive(b, k, n)
                        if n - 3 in POOL_N:
                            product(b, k, n - 3)
                    if k < NK - 1 and scan:
                        if n == 11:
                            lost(b, k + 1)
                        if n == 12:
                            log1p(b, k + 1)
                        if n == 14:
                            dt_u(b, k + 1)
                    if k == NK - 1 and pre:
                        if n == 11:
                            lost(b + 1, 0)
                        if n == 12:
                            log1p(b + 1, 0)
                        if n == 14:
                            dt_u(b + 1, 0)
                    if s == 16 and post:
                        inverse_std(b - 1, mv1, Mv1, var1, Rs1, rs1, 1)
                    if s == 63 and post:
                        inverse_std(b - 1, mv2, Mv2, var2, Rs2, rs2, 0)

            pool.wait_ge(w_ready, 1)
            batches(pool, iteration)

        @block.vector
        def _(dve):
            def taps(b, j):
                reach(dve, xi_copied, b, NK, j + 1)
                for t in reversed(range(TAPS - 1)):
                    reach(dve, tap_done, b, NK * (TAPS - 1), j * (TAPS - 1) + TAPS - 2 - t)
                    c = U[:, b.parity, j, :]
                    ins = nc.vector.scalar_tensor_tensor(c, Xi[:, t:t + SEQ], ConvW[:, j, t:t + 1], c,
                                                         ALU.mult, ALU.add)
                    ins.then_inc(tap_done, 1)

            def u(b, j):
                reach(dve, tanh_c, b, NK, j + 1)
                c = U[:, b.parity, j, :]
                nc.vector.scalar_tensor_tensor(c, TanhC[:, :], 1.0, c, ALU.add, ALU.mult).then_inc(u_ready, 1)

            def split_rest(b, part):
                if part == 0:
                    reach(dve, split_hi, b, 1, 1)
                    nc.vector.tensor_tensor(Dbl[0:BC_PARTS, :], W["C"][0:BC_PARTS, :], DblS[:, :],
                                            ALU.subtract).then_inc(rest1, 1)
                else:
                    reach(dve, split_mid, b, 1, 1)
                    nc.vector.tensor_tensor(Dbl[64:96, :], Dbl[64:96, :], DblS[64:96, :],
                                            ALU.subtract).then_inc(rest2, 1)

            def rounded(b, k):
                reach(dve, sp_e, b, NK, k + 1)
                reach(dve, dt_ready, b, NK, k)
                nc.vector.tensor_scalar(Sp_fix[:, :], Sp_e[:, :], 1.0, -1.0, ALU.add, ALU.add).then_inc(sp_rounded, 1)

            def dt(b, k):
                reach(dve, sp_sum, b, NK, k + 1)
                reach(dve, dA_ready, b, UNITS, (k - 1) * NS)
                reach(dve, dtu_ready, b, NK, k - 1)
                nc.vector.tensor_tensor(Dt[:, k % 2, :], Sp_fix[:, :], Sp_relu[:, :], ALU.add).then_inc(dt_ready, 1)

            def scan_unit(b, k, n):
                unit = k * NS + n
                reach(dve, dA_ready, b, UNITS, unit + 1)
                reach(dve, dBu_ready, b, UNITS, unit + 1)
                if n in POOL_N:
                    reach(dve, prod_pool, b, NK * len(POOL_N), k * len(POOL_N) + POOL_N.index(n))
                    h = Hs
                else:
                    reach(dve, prod_vec, b, NK * len(VEC_N), vec_count(unit - 1))
                    h = H[unit % 2]
                nc.vector.tensor_tensor_scan(h[:, :], dA[unit % 2][:, :], DBu[:, unit % DBU_RING, :], 0.0,
                                             ALU.mult, ALU.add).then_inc(h_ready, 1)

            def product(b, k, n):
                unit = k * NS + n
                reach(dve, h_ready, b, UNITS, unit + 1)
                if k == 0:
                    reach(dve, C_ready, b, NS, n + 1)
                reach(dve, y_added, b, UNITS, prod_slot_free(unit))
                nc.vector.tensor_tensor(Prod[:, unit % PROD_RING, :], H[unit % 2][:, :], Cc[:, n, :],
                                        ALU.mult).then_inc(prod_vec, 1)

            def z_silu(b, k):
                reach(dve, tanh_z, b, NK, k + 1)
                flat = G[:, :, :].rearrange("p t d -> p (t d)")
                nc.vector.scalar_tensor_tensor(flat, flat, 1.0, W["C"][:, :], ALU.add, ALU.mult).then_inc(silu_z, 1)

            def gated(b, k):
                reach(dve, y_added, b, UNITS, (k + 1) * NS)
                dve.wait_ge(silu_z, b.times(NK, k + 1))
                flat = G[:, :, :].rearrange("p t d -> p (t d)")
                nc.vector.tensor_tensor(flat, Y[:, :], flat, ALU.mult).then_inc(g_ready, 1)

            def mix_terms(b, half):
                if half == 0:
                    dve.wait_ge(xn_loaded, b.times(16, 16))
                    reach(dve, stored, b, 16, ONE)
                rows = slice(2 * half, 2 * half + 2)
                reach(dve, tanh_f, b, 2, half + 1)
                nc.vector.scalar_tensor_tensor(X1[:, rows, :], TanhF[:, rows, :], 3.0, XN[:, rows, :],
                                               ALU.add, ALU.mult).then_inc(mix_parts, 1)
                reach(dve, nf_done, b, 2, half + 1)
                dve.wait_ge(mix_parts, b.times(4, 2 * half + 1))
                nc.vector.scalar_tensor_tensor(TanhF[:, rows, :], TanhF[:, rows, :], -1.0,
                                               W["A"][:, :].rearrange("p (t d) -> p t d", t=2),
                                               ALU.add, ALU.mult).then_inc(mix_parts, 1)

            def mix(b, half):
                rows = slice(2 * half, 2 * half + 2)
                dve.wait_ge(mix_parts, b.times(4, 2 * half + 2))
                nc.vector.tensor_tensor(X1[:, rows, :], X1[:, rows, :], TanhF[:, rows, :],
                                        ALU.subtract).then_inc(mixed, 1)
                statistics(b, half, mixed, Stats1, stats1)

            def statistics(b, half, source, Stats, stats):
                dve.wait_ge(source, b.times(2, half + 1))
                for t in (2 * half, 2 * half + 1):
                    nc.vector.bn_stats(Stats[:, t, :], X1[:, t, :]).then_inc(stats, 1)

            def aggregate(Stats, Mv, mv, half):
                for t in (2 * half, 2 * half + 1):
                    nc.vector.bn_aggr(Mv[:, t, :], Stats[:, t, :]).then_inc(mv, 1)

            def normalize(b, rs, Mv, Rs, ready):
                reach(dve, rs, b, 1, 1)
                for t in range(TB):
                    ins = nc.vector.tensor_scalar(X1[:, t, :], X1[:, t, :], Mv[:, t, 0:1], Rs[:, t:t + 1],
                                                  ALU.subtract, ALU.mult)
                ins.then_inc(ready, 1)

            def gate_silu(b, c):
                reach(dve, tanh_g, b, NC, c + 1)
                nc.vector.scalar_tensor_tensor(Ht[:, c, :], Ht[:, c, :], 1.0, W["A"][:, :],
                                               ALU.add, ALU.mult).then_inc(silu_g, 1)

            def gate_up(b, c):
                reach(dve, up_done, b, NC, ONE + c + 1)
                dve.wait_ge(silu_g, b.times(NC, c + 1))
                nc.vector.tensor_tensor(Ht[:, c, :], W["B"][:, :], Ht[:, c, :], ALU.mult).then_inc(hid_ready, 1)

            def residual(b, half):
                rows = slice(2 * half, 2 * half + 2)
                reach(dve, down_done, b, 2, ONE + half + 1)
                nc.vector.tensor_tensor(X1[:, rows, :], W["C"][:, :].rearrange("p (t d) -> p t d", t=2),
                                        X1[:, rows, :], ALU.add).then_inc(summed, 1)
                statistics(b, half, summed, Stats2, stats2)

            def last_product(b):
                product(b, NK - 1, NS - 1)

            def iteration(b):
                post, scan, pre = has_post(b), has_scan(b), has_pre(b)
                for s in range(UNITS):
                    k, n = divmod(s, NS)
                    if s in (11, 13) and post:
                        reach(dve, stats1, b - 1, TB, s - 9)
                    if s in (57, 60) and post:
                        reach(dve, stats2, b - 1, TB, 2 if s == 57 else 4)
                    if scan:
                        scan_unit(b, k, n)
                    if s in (11, 13) and post:
                        aggregate(Stats1, Mv1, mv1, (s - 11) // 2)
                    if s in (57, 60) and post:
                        aggregate(Stats2, Mv2, mv2, (s - 57) // 3)
                    if s == 0 and post:
                        last_product(b - 1)
                    if scan and s and (s - 1) % NS not in POOL_N:
                        product(b, *divmod(s - 1, NS))
                    if s == 2 and post:
                        gated(b - 1, NK - 1)
                    if n == 2 and k and scan:
                        gated(b, k - 1)
                    if n == 8 and k < NK - 1 and scan:
                        rounded(b, k + 1)
                    if n == 12 and k < NK - 1 and scan:
                        dt(b, k + 1)
                    if s == 56 and pre:
                        rounded(b + 1, 0)
                    if s == 60 and pre:
                        dt(b + 1, 0)
                    if n == 14 and scan:
                        z_silu(b, k)
                    if s in (9, 11) and post:
                        mix_terms(b - 1, (s - 9) // 2)
                    if s in (10, 12) and post:
                        mix(b - 1, (s - 10) // 2)
                    if s == 15 and post:
                        normalize(b - 1, rs1, Mv1, Rs1, x1_ready)
                    if s - 4 in XI_SLOTS and pre:
                        taps(b + 1, XI_SLOTS.index(s - 4))
                    if s - 8 in XI_SLOTS and pre:
                        u(b + 1, XI_SLOTS.index(s - 8))
                    if s - 4 in GATE_SLOTS and post:
                        gate_silu(b - 1, GATE_SLOTS.index(s - 4))
                    if s - 5 in GATE_SLOTS and post:
                        gate_up(b - 1, GATE_SLOTS.index(s - 5))
                    if s in (41, 44) and pre:
                        split_rest(b + 1, (s - 41) // 3)
                    if s in (56, 59) and post:
                        residual(b - 1, (s - 56) // 3)
                    if s == 63 and post:
                        normalize(b - 1, rs2, Mv2, Rs2, out_ready)

            nc.vector.memset(Xi[:, 0:TAPS - 1], 0.0)
            nc.vector.memset(Ones[:, :], 1.0).then_inc(stored, ONE)
            nc.vector.memset(MinusHalf[:, :], -0.5).then_inc(down_done, ONE)
            nc.vector.memset(Eps[:, 0, :], EPS).then_inc(gate_done, ONE)
            nc.vector.memset(Eps[:, 1, :], 4 * EPS).then_inc(up_done, ONE)
            nc.vector.memset(Dbl[DT_ROW:P, :], 1.0)
            dve.wait_ge(w_loaded, 16 * LOADS)
            nc.vector.tensor_scalar(ConvW[:, :, :], ConvW[:, :, :], 0.5, None, ALU.mult)
            nc.vector.tensor_scalar(ConvB[:, :], ConvB[:, :], 0.5, None, ALU.mult)
            nc.vector.tensor_copy(Sel[:, :, :], Eye3[:, :].unsqueeze(2).broadcast_to([BC_PARTS, 2 * NS, P]))
            for k in range(NK):
                nc.vector.tensor_scalar(DiagD[:, k, :], Id[:, :], Dcol[:, k:k + 1], None, ALU.mult)
            nc.vector.tensor_scalar(Wgate[:, :, :].rearrange("p k n -> p (k n)"), gate_stage, DEQUANT, None, ALU.mult)
            nc.vector.tensor_scalar(Wup[:, :, :].rearrange("p k n -> p (k n)"), up_stage, DEQUANT, None, ALU.mult)
            nc.vector.tensor_scalar(Wdown[:, :, :].rearrange("p k n -> p (k n)"), down_stage, DEQUANT, 0.5,
                                    ALU.mult, ALU.mult)
            dve.wait_ge(a_ready, 1)
            nc.vector.tensor_scalar(NegA[:, :, :], NegA[:, :, :], -1.0, None, ALU.mult).then_inc(w_ready, 1)
            dve.wait_ge(w_ready, 1)
            batches(dve, iteration)


LOADS = 19
XI_SLOTS = [9, 12, 15, 19]
GATE_SLOTS = [22 + 4 * c for c in range(NC)]
DOWN_SLOTS = [52, 53, 55, 56]


def vec_count(units):
    whole, part = divmod(units, NS)
    return whole * len(VEC_N) + sum(n < part for n in VEC_N)


def prod_slot_free(unit):
    if unit >= PROD_RING:
        return unit + 1 - PROD_RING
    last = max(v for v in range(UNITS) if v % PROD_RING == unit)
    return last + 1 - UNITS


def kernel(**inputs):
    import numpy as np
    import concourse.bacc as bacc
    from concourse.bass_utils import run_bass_kernel_spmd

    a = {n.replace("L0_attn_", "").replace("L0_ffn_", ""): np.asarray(v) for n, v in inputs.items()}
    eye = np.eye(P, dtype=np.float32)
    eye_bc = np.eye(2 * NS, dtype=np.float32)
    arrays = {
        "x": a["x"].reshape(BATCH * SEQ, DM),
        "xT": a["x"].transpose(0, 2, 1).reshape(BATCH * DM, SEQ),
        "in_w": a["in_proj_w"],
        "conv_w": a["conv_w"],
        "conv_b": a["conv_b"].reshape(NK, P).T,
        "xp_w": a["x_proj_w"],
        "dt_w": a["dt_proj_w"],
        "dt_b": a["dt_proj_b"],
        "a_log": a["A_log"],
        "d_skip": a["D"].reshape(NK, P).T,
        "out_w": a["out_proj_w"],
        "fg_w": a["fg_w"],
        "fg_b": a["fg_b"],
        "gate_wT": a["w_gate"].T,
        "up_wT": a["w_up"].T,
        "down_wT": a["w_down"].T,
        "ident": eye,
        "eye3": np.concatenate([eye_bc, eye_bc, eye_bc]),
    }
    nc = bacc.Bacc("TRN2", target_bir_lowering=False, num_devices=1)
    args = {}
    for name, v in arrays.items():
        arrays[name] = np.ascontiguousarray(v)
        args[name] = nc.dram_tensor(f"in_{name}", v.shape, mybir.dt.from_np(v.dtype), kind="ExternalInput").ap()
    out = nc.dram_tensor("out_dram", (BATCH * SEQ, DM), F32, kind="ExternalOutput").ap()
    build(nc, *args.values(), out)
    r = run_bass_kernel_spmd(nc, [{f"in_{n}": v for n, v in arrays.items()}], core_ids=[0])
    return r.results[0]["out_dram"].reshape(BATCH, SEQ, DM)
```

```python
from contextlib import ExitStack

import concourse.bass as bass
from concourse import mybir

F32 = mybir.dt.float32
BF16 = mybir.dt.bfloat16
I32 = mybir.dt.int32
ALU = mybir.AluOpType
ACT = mybir.ActivationFunctionType

BATCH, SEQ, DM = 8, 512, 256
DI, NS, TAPS, RANK = 512, 16, 4, 16
HID = 768
P = 128
NK = DI // P
KM = DM // P
TB = SEQ // P
NC = HID // P
UNITS = NK * NS
EPS = 1e-5
DEQUANT = 1.0 / 127.0

POOL_N = (2, 5, 12)
VEC_N = [n for n in range(NS) if n not in POOL_N]
DBU_RING, PROD_RING = 4, 4
ONE = 1
BC_PARTS = 96
DT_ROW = 96

TRIPS = (BATCH - 2) // 2

class Batch:

    def __init__(self, const, trip=None):
        self.const, self.trip = const, trip

    def __add__(self, d):
        return Batch(self.const + d, self.trip)

    def __sub__(self, d):
        return Batch(self.const - d, self.trip)

    @property
    def parity(self):
        return self.const % 2

    def times(self, per, extra=0):
        if self.trip is None:
            return per * self.const + extra
        return self.trip * (2 * per) + (per * self.const + extra)


def reach(eng, sem, b, per, extra):
    if per * b.const + extra <= 0:
        assert b.trip is None
        return
    eng.wait_ge(sem, b.times(per, extra))


def batches(eng, iteration):
    iteration(Batch(0))
    with eng.Fori(0, TRIPS) as trip:
        for c in (1, 2):
            iteration(Batch(c, trip))
    for c in (BATCH - 1, BATCH):
        iteration(Batch(c))


def has_post(b):
    return b.trip is not None or b.const >= 1


def has_scan(b):
    return b.trip is not None or 0 <= b.const < BATCH


def has_pre(b):
    return b.trip is not None or b.const < BATCH - 1


def build(nc, x, xT, in_w, conv_w, conv_b, xp_w, dt_w, dt_b, a_log, d_skip, out_w, fg_w, fg_b,
          gate_wT, up_wT, down_wT, ident, eye3, out):
    ctx = ExitStack()
    with ctx:
        def sb(name, shape, dt=F32):
            return ctx.enter_context(nc.sbuf_tensor(name, shape, dt))

        def ps(name):
            return ctx.enter_context(nc.psum_tensor(name, [P, SEQ], F32))

        def sem(name):
            return ctx.enter_context(nc.semaphore(name))

        Win = sb("Win", [P, KM, 2 * DI])
        Wxp = sb("Wxp", [P, NK, BC_PARTS + RANK])
        Wout = sb("Wout", [P, NK, DM])
        Wfg = sb("Wfg", [P, KM, DM])
        FgS = sb("FgS", [BC_PARTS, 2 * DM], BF16)
        Wgate = sb("Wgate", [P, KM, HID])
        Wup = sb("Wup", [P, KM, HID])
        Wdown = sb("Wdown", [P, NC, DM])
        Id = sb("Id", [P, P])
        Eye3 = sb("Eye3", [BC_PARTS, 2 * NS])
        SelDt = sb("SelDt", [P, 2 * NS, P], BF16)
        Sel = SelDt[0:BC_PARTS, :, :]
        Wdt = SelDt[:, 0:2 * DI // P, :].rearrange("p r c -> p (r c)").bitcast(F32)
        DiagD = sb("DiagD", [P, NK, P])
        ConvW = sb("ConvW", [P, NK, TAPS])
        ConvB = sb("ConvB", [P, NK])
        Dcol = sb("Dcol", [P, NK])
        NegA = sb("NegA", [P, NK, NS])
        Ones = sb("Ones", [BC_PARTS, P], BF16)
        MinusHalf = sb("MinusHalf", [P, TB])
        Eps = sb("Eps", [P, 2, TB])

        XT = sb("XT", [P, 2, KM, SEQ])
        XN = sb("XN", [P, TB, DM])
        Bc = sb("Bc", [P, NS, SEQ])
        Cc = sb("Cc", [P, NS, SEQ])
        Xi = sb("Xi", [P, TAPS - 1 + SEQ])
        U = sb("U", [P, 2, NK, SEQ])
        TanhC = sb("TanhC", [P, SEQ])
        DblS = sb("DblS", [BC_PARTS, SEQ], BF16)
        Dbl = sb("Dbl", [P, SEQ])
        Sp_e = sb("Sp_e", [P, SEQ])
        Sp_ln = sb("Sp_ln", [P, SEQ])
        Sp_1e = sb("Sp_1e", [P, SEQ])
        Dt = sb("Dt", [P, 2, SEQ])
        DtU = sb("DtU", [P, 2, SEQ])
        DBu = sb("DBu", [P, DBU_RING, SEQ])
        Prod = sb("Prod", [P, PROD_RING, SEQ])
        Hs = sb("Hs", [P, SEQ])
        G = sb("G", [P, TB, P])
        Gt = sb("Gt", [P, NK, SEQ])
        TanhF = sb("TanhF", [P, TB, DM])
        X1 = sb("X1", [P, TB, DM])
        Ht = sb("Ht", [P, NC, SEQ])
        Stats1 = sb("Stats1", [P, TB, 6])
        Mv1 = sb("Mv1", [P, TB, 2])
        Rs1 = sb("Rs1", [P, TB])
        Stats2 = sb("Stats2", [P, TB, 6])
        Mv2 = sb("Mv2", [P, TB, 2])
        Rs2 = sb("Rs2", [P, TB])
        X1t = Gt[:, 2:4, :]

        dA = [ps(f"dA{i}") for i in range(2)]
        H = [ps(f"H{i}") for i in range(2)]
        Y = ps("Y")
        W = {name: ps(f"work{name}") for name in "ABC"}

        w_in = sem("w_in")
        w_scan = sem("w_scan")
        w_post = sem("w_post")
        xt_loaded = [sem(f"xt_loaded{i}") for i in range(2)]
        xn_loaded = sem("xn_loaded")
        stored = sem("stored")
        conv_ready = sem("conv_ready")
        const_ready = sem("const_ready")
        ffn_ready = sem("ffn_ready")
        fgb_loaded = sem("fgb_loaded")
        fgb_split = sem("fgb_split")
        a_exp = sem("a_exp")
        a_ready = sem("a_ready")
        xi_done = sem("xi_done")
        xi_copied = sem("xi_copied")
        tap_done = sem("tap_done")
        tanh_c = sem("tanh_c")
        u_ready = sem("u_ready")
        dbl_done = sem("dbl_done")
        split_hi = sem("split_hi")
        rest1 = sem("rest1")
        split_mid = sem("split_mid")
        rest2 = sem("rest2")
        split_lo = sem("split_lo")
        bcB_done, bcC_done = sem("bcB_done"), sem("bcC_done")
        B_ready, C_ready = sem("B_ready"), sem("C_ready")
        v_done = sem("v_done")
        sp_abs = sem("sp_abs")
        sp_e = sem("sp_e")
        sp_1e = sem("sp_1e")
        sp_ln = sem("sp_ln")
        sp_gain = sem("sp_gain")
        sp_sum = sem("sp_sum")
        dt_ready = sem("dt_ready")
        dtu_ready = sem("dtu_ready")
        dA_ready = sem("dA_ready")
        dBu_ready = sem("dBu_ready")
        h_ready = sem("h_ready")
        prod_vec = sem("prod_vec")
        prod_pool = sem("prod_pool")
        y_added = sem("y_added")
        z_done = sem("z_done")
        tanh_z = sem("tanh_z")
        silu_z = sem("silu_z")
        g_ready = sem("g_ready")
        gt_done = sem("gt_done")
        gt_copied = sem("gt_copied")
        fg_done = sem("fg_done")
        tanh_f = sem("tanh_f")
        nf_done = sem("nf_done")
        mix_parts = sem("mix_parts")
        mixed = sem("mixed")
        stats1 = sem("stats1")
        mv1 = sem("mv1")
        var1 = sem("var1")
        rs1 = sem("rs1")
        x1_ready = sem("x1_ready")
        x1t_done = sem("x1t_done")
        x1t_copied = sem("x1t_copied")
        gate_done, up_done = sem("gate_done"), sem("up_done")
        tanh_g = sem("tanh_g")
        silu_g = sem("silu_g")
        hid_ready = sem("hid_ready")
        down_done = sem("down_done")
        summed = sem("summed")
        stats2 = sem("stats2")
        mv2 = sem("mv2")
        var2 = sem("var2")
        rs2 = sem("rs2")
        out_ready = sem("out_ready")

        gate_stage = Ht[:, 0:3, :].rearrange("p a b -> p (a b)").bitcast(I32)
        up_stage = Ht[:, 3:6, :].rearrange("p a b -> p (a b)").bitcast(I32)
        down_stage = Gt[:, 0:3, :].rearrange("p a b -> p (a b)").bitcast(I32)

        fgb_stage = TanhF[0:BC_PARTS, 0:2, :].rearrange("p t d -> p (t d)")

        block = ctx.enter_context(nc.Block())

        @block.sync
        def _(sp):
            def rows(dram, b, count):
                if b.trip is None:
                    return dram[b.times(count):b.times(count) + count, :]
                return dram[bass.ds(sp.snap(b.times(count)), count), :]

            bc_w = xp_w[:, RANK:RANK + 2 * NS].rearrange("(k p) n -> p k n", p=P)
            loads = {
                w_in: [
                    (Win[:, :, 0:DI], in_w[:, 0:DI].rearrange("(k p) n -> p k n", p=P)),
                    (ConvW[:, :, :], conv_w.rearrange("(k p) o t -> p k (o t)", p=P)),
                    (ConvB[:, :], conv_b),
                ],
                w_scan: [
                    (Wxp[:, :, 0:32], bc_w), (Wxp[:, :, 32:64], bc_w), (Wxp[:, :, 64:96], bc_w),
                    (Wxp[:, :, 96:96 + RANK], xp_w[:, 0:RANK].rearrange("(k p) n -> p k n", p=P)),
                    (Wdt[DT_ROW:DT_ROW + RANK, :], dt_w),
                    (Wdt[DT_ROW + RANK:DT_ROW + RANK + 1, :], dt_b.rearrange("(o n) -> o n", o=1)),
                    (Dcol[:, :], d_skip),
                    (Id[:, :], ident),
                    (Eye3[:, :], eye3),
                    (NegA[:, :, :], a_log.rearrange("(k p) n -> p k n", p=P)),
                    (Win[:, :, DI:], in_w[:, DI:].rearrange("(k p) n -> p k n", p=P)),
                ],
                w_post: [
                    (Wfg[:, :, :], fg_w.rearrange("(k p) n -> p k n", p=P)),
                    (Wout[:, :, :], out_w.rearrange("(k p) n -> p k n", p=P)),
                    (gate_stage.rearrange("p (k n) -> p k n", k=KM), gate_wT.rearrange("(k p) n -> p k n", p=P)),
                    (up_stage.rearrange("p (k n) -> p k n", k=KM), up_wT.rearrange("(k p) n -> p k n", p=P)),
                    (down_stage.rearrange("p (k n) -> p k n", k=NC), down_wT.rearrange("(k p) n -> p k n", p=P)),
                ],
            }

            def load_xt(b, source):
                sp.dma_start(XT[:, b.parity, :, :], source.rearrange("(k p) t -> p k t", p=P)
                             ).then_inc(xt_loaded[b.parity], 16)

            load_xt(Batch(0), rows(xT, Batch(0), KM * P))
            for loaded, parts in loads.items():
                assert len(parts) == LOADS[loaded.name]
                for dst, src in parts:
                    sp.dma_start(dst, src).then_inc(loaded, 16)

            def iteration(b):
                if has_scan(b) and has_pre(b):
                    source = rows(xT, b + 1, KM * P)
                    reach(sp, z_done, b - 1, NK, NK)
                    load_xt(b + 1, source)
                if has_scan(b):
                    source = rows(x, b, SEQ)
                    reach(sp, mixed, b - 1, 2, 2)
                    sp.dma_start(XN[:, :, :], source.rearrange("(t p) d -> p t d", p=P)).then_inc(xn_loaded, 16)
                if has_post(b):
                    target = rows(out, b - 1, SEQ)
                    reach(sp, out_ready, b - 1, 1, 1)
                    sp.dma_start(target.rearrange("(t p) d -> p t d", p=P), X1[:, :, :]).then_inc(stored, 16)

            sp.wait_ge(fgb_split, 1)
            for row in (0, 32, 64):
                for half in (0, 1):
                    sp.dma_start(fgb_stage[row:row + 1, half * DM:(half + 1) * DM],
                                 fg_b.rearrange("(o n) -> o n", o=1)).then_inc(fgb_loaded, 16)
            iteration(Batch(-1))
            batches(sp, iteration)
            sp.wait_ge(stored, 16 * BATCH + ONE)

        @block.tensor
        def _(pe):
            read_by = {name: None for name in W}

            def take(name, sem, b, per, extra):
                if read_by[name]:
                    before, when, *count = read_by[name]
                    pe.wait_ge(before, when.times(*count))
                read_by[name] = (sem, b, per, extra)
                return W[name]

            def xi(b, j):
                if j == 0:
                    before = 16 * (b.const // 2)
                    pe.wait_ge(xt_loaded[b.parity], before + 16 if b.trip is None else b.trip * 16 + (before + 16))
                bank = take(BANK["xi"][j], xi_copied, b, NK, j + 1)
                for k in range(KM):
                    mm = nc.tensor.matmul(bank[:, :], Win[:, k, j * P:(j + 1) * P], XT[:, b.parity, k, :],
                                          start=(k == 0), stop=(k == KM - 1))
                mm.then_inc(xi_done, 1)

            def x_proj(b):
                if b.trip is None and b.const == 0:
                    pe.wait_ge(w_scan, 16 * LOADS["w_scan"])
                    pe.wait_ge(const_ready, 1)
                bank = take(BANK["x_proj"], rest1, b, 1, 1)
                reach(pe, u_ready, b, NK, NK)
                for k in range(NK):
                    mm = nc.tensor.matmul(bank[0:BC_PARTS + RANK, :], Wxp[:, k, :], U[:, b.parity, k, :],
                                          start=(k == 0), stop=(k == NK - 1))
                mm.then_inc(dbl_done, 1)

            def broadcast(b, n):
                if n == 0:
                    reach(pe, split_lo, b, 1, 1)
                for name, row, done, ready in (("A", n, bcB_done, B_ready), ("B", NS + n, bcC_done, C_ready)):
                    bank = take(name, ready, b, NS, n + 1)
                    nc.tensor.matmul(bank[:, :], Sel[:, row, :], DblS[:, :], start=True, stop=True).then_inc(done, 1)

            def dt_arg(b, k):
                bank = take(BANK["v"], sp_abs, b, NK, k + 1)
                if k == 0:
                    reach(pe, split_hi, b, 1, 1)
                rows = slice(DT_ROW, DT_ROW + RANK + 1)
                nc.tensor.matmul(bank[:, :], Wdt[rows, k * P:(k + 1) * P], Dbl[rows, :],
                                 start=True, stop=True).then_inc(v_done, 1)

            def z(b, k):
                bank = take(BANK["z"], silu_z, b, NK, k + 1)
                for t in range(TB):
                    for c in range(KM):
                        mm = nc.tensor.matmul(bank[:, t * P:(t + 1) * P], XT[:, b.parity, c, t * P:(t + 1) * P],
                                              Win[:, c, DI + k * P:DI + (k + 1) * P],
                                              start=(c == 0), stop=(c == KM - 1))
                mm.then_inc(z_done, 1)

            def feature_gate(b, half):
                if b.trip is None and b.const == 0 and half == 0:
                    pe.wait_ge(fgb_split, FGB_STEPS)
                bank = take(BANK["fg"][half], tanh_f, b, 2, half + 1)
                nc.tensor.matmul(bank[:, :], Ones[:, :], FgS[:, :], start=True, stop=False, skip_group_check=True)
                for t in range(2):
                    rows = slice((2 * half + t) * P, (2 * half + t + 1) * P)
                    for c in range(KM):
                        mm = nc.tensor.matmul(bank[:, t * DM:(t + 1) * DM], XT[:, b.parity, c, rows], Wfg[:, c, :],
                                              start=False, stop=(c == KM - 1), skip_group_check=True)
                mm.then_inc(fg_done, 1)

            def y_skip(b, k):
                if k or has_post(b):
                    reach(pe, g_ready, b, NK, k)
                for t in range(TB):
                    nc.tensor.matmul(Y[:, t * P:(t + 1) * P], U[:, b.parity, k, t * P:(t + 1) * P], DiagD[:, k, :],
                                     start=(t == 0), stop=False, skip_group_check=True)

            def y_add(b, k, n):
                unit = k * NS + n
                if n in POOL_N:
                    reach(pe, prod_pool, b, NK * len(POOL_N), k * len(POOL_N) + POOL_N.index(n) + 1)
                else:
                    reach(pe, prod_vec, b, NK * len(VEC_N), k * len(VEC_N) + VEC_N.index(n) + 1)
                slot = unit % PROD_RING
                for t in range(TB):
                    mm = nc.tensor.matmul(Y[:, t * P:(t + 1) * P], Prod[:, slot, t * P:(t + 1) * P], Id[:, :],
                                          start=False, stop=(n == NS - 1), is_transpose=True,
                                          skip_group_check=True)
                mm.then_inc(y_added, 1)

            def g_transpose(b, k):
                bank = take(BANK["gt"], gt_copied, b, NK, k + 1)
                reach(pe, g_ready, b, NK, k + 1)
                for t in range(TB):
                    mm = nc.tensor.transpose(bank[:, t * P:(t + 1) * P], G[:, t, :], Id[:, :])
                mm.then_inc(gt_done, 1)

            def out_proj(b, t):
                if t == 0:
                    reach(pe, gt_copied, b, NK, NK)
                if t % 2 == 0:
                    take(BANK["nf"][t // 2], mix_parts, b, 4, t + 2)
                for c in range(NK):
                    mm = nc.tensor.matmul(W[BANK["nf"][t // 2]][:, (t % 2) * DM:(t % 2 + 1) * DM], Gt[:, c, t * P:(t + 1) * P],
                                          Wout[:, c, :], start=(c == 0), stop=(c == NK - 1))
                if t % 2:
                    mm.then_inc(nf_done, 1)

            def x1_transpose(b, c):
                bank = take(BANK["x1t"][c], x1t_copied, b, KM, c + 1)
                if c == 0:
                    reach(pe, x1_ready, b, 1, 1)
                for t in range(TB):
                    mm = nc.tensor.transpose(bank[:, t * P:(t + 1) * P], X1[:, t, c * P:(c + 1) * P], Id[:, :])
                mm.then_inc(x1t_done, 1)

            def hidden(b, c, name, weights, done, read):
                bank = take(name, read, b, NC, c + 1)
                if c == 0:
                    reach(pe, x1t_copied, b, KM, KM)
                for k in range(KM):
                    mm = nc.tensor.matmul(bank[:, :], weights[:, k, c * P:(c + 1) * P], X1t[:, k, :],
                                          start=(k == 0), stop=(k == KM - 1))
                mm.then_inc(done, 1)

            def down(b, t):
                if t == 0:
                    reach(pe, hid_ready, b, NC, NC)
                if t % 2 == 0:
                    take(BANK["down"][t // 2], summed, b, 2, t // 2 + 1)
                for c in range(NC):
                    mm = nc.tensor.matmul(W[BANK["down"][t // 2]][:, (t % 2) * DM:(t % 2 + 1) * DM], Ht[:, c, t * P:(t + 1) * P],
                                          Wdown[:, c, :], start=(c == 0), stop=(c == NC - 1))
                if t % 2:
                    mm.then_inc(down_done, 1)

            def iteration(b):
                post, scan, pre = has_post(b), has_scan(b), has_pre(b)
                for s in range(UNITS):
                    k, n = divmod(s, NS)
                    if scan and n == PE_AT["open"]:
                        y_skip(b, k)
                        for first in range(n):
                            y_add(b, k, first)
                    if scan and n >= PE_AT["open"]:
                        y_add(b, k, n)
                    if scan and 0 <= s + UNITS - PE_AT["bc"] < NS:
                        broadcast(b, s + UNITS - PE_AT["bc"])
                    if n == PE_AT["gt"] and (scan if k else post):
                        g_transpose(*((b, k - 1) if k else (b - 1, NK - 1)))
                    if n == PE_AT["v"] and k < NK - 1 and scan:
                        dt_arg(b, k + 1)
                    if s == PE_AT["v0"] and pre:
                        dt_arg(b + 1, 0)
                    if n == PE_AT["z"] and scan:
                        z(b, k)
                    if post:
                        for t in steps(PE_AT, "nf", s):
                            out_proj(b - 1, t)
                        for c in steps(PE_AT, "x1t", s):
                            x1_transpose(b - 1, c)
                        for c in steps(PE_AT, "gate", s):
                            hidden(b - 1, c, "A", Wgate, gate_done, silu_g)
                        for c in steps(PE_AT, "up", s):
                            hidden(b - 1, c, "B", Wup, up_done, hid_ready)
                        for t in steps(PE_AT, "down", s):
                            down(b - 1, t)
                    if scan:
                        for half in steps(PE_AT, "fg", s):
                            feature_gate(b, half)
                    if pre:
                        for c in steps(PE_AT, "xi", s):
                            xi(b + 1, c)
                        if s == PE_AT["x_proj"]:
                            x_proj(b + 1)
                        if 0 <= s - PE_AT["bc"] < NS:
                            broadcast(b + 1, s - PE_AT["bc"])

            pe.wait_ge(w_in, 16 * LOADS["w_in"])
            iteration(Batch(-1))
            pe.wait_ge(w_post, 16 * LOADS["w_post"])
            iteration(Batch(0))
            pe.wait_ge(ffn_ready, 1)
            with pe.Fori(0, TRIPS) as trip:
                for name, (sem_, b, *count) in read_by.items():
                    read_by[name] = (sem_, Batch(b.const, trip), *count)
                for c in (1, 2):
                    iteration(Batch(c, trip))
            for name, (sem_, b, *count) in read_by.items():
                read_by[name] = (sem_, Batch(b.const + 2 * (TRIPS - 1)), *count)
            for c in (BATCH - 1, BATCH):
                iteration(Batch(c))

        @block.scalar
        def _(act):
            def xi_copy(b, j):
                reach(act, xi_done, b, NK, j + 1)
                reach(act, tap_done, b, NK * (TAPS - 1), j * (TAPS - 1))
                reach(act, y_added, b - 2, UNITS, UNITS)
                reach(act, dtu_ready, b - 2, NK, NK)
                bank = W[BANK["xi"][j]]
                nc.scalar.activation(Xi[:, TAPS - 1:], bank[:, :], ACT.Copy)
                nc.scalar.activation(U[:, b.parity, j, :], bank[:, :], ACT.Identity, bias=ConvB[:, j:j + 1],
                                     scale=ConvW[:, j, TAPS - 1:TAPS]).then_inc(xi_copied, 1)

            def xi_tanh(b, j):
                reach(act, tap_done, b, NK * (TAPS - 1), (j + 1) * (TAPS - 1))
                reach(act, u_ready, b, NK, j)
                nc.scalar.activation(TanhC[:, :], U[:, b.parity, j, :], ACT.Tanh).then_inc(tanh_c, 1)

            def split(b, part):
                if part == 0:
                    reach(act, dbl_done, b, 1, 1)
                    reach(act, bcC_done, b, NS, 0)
                    reach(act, v_done, b, NK, 0)
                    reach(act, split_lo, b, 1, 0)
                    rows = slice(DT_ROW, DT_ROW + RANK)
                    nc.scalar.activation(Dbl[rows, :], W[BANK["x_proj"]][rows, :], ACT.Copy)
                    nc.scalar.activation(DblS[:, :], W[BANK["x_proj"]][0:BC_PARTS, :], ACT.Copy).then_inc(split_hi, 1)
                elif part == 1:
                    reach(act, rest1, b, 1, 1)
                    nc.scalar.activation(DblS[32:64, :], Dbl[32:64, :], ACT.Copy)
                    nc.scalar.activation(DblS[64:96, :], Dbl[64:96, :], ACT.Copy).then_inc(split_mid, 1)
                else:
                    reach(act, rest2, b, 1, 1)
                    nc.scalar.activation(DblS[64:96, :], Dbl[64:96, :], ACT.Copy).then_inc(split_lo, 1)

            def bc_copy(b, n):
                last = NK - 1
                reach(act, bcB_done, b, NS, n + 1)
                reach(act, dBu_ready, b - 1, UNITS, last * NS + n + 1)
                nc.scalar.activation(Bc[:, n, :], W["A"][:, :], ACT.Copy).then_inc(B_ready, 1)
                reach(act, bcC_done, b, NS, n + 1)
                if n in POOL_N:
                    reach(act, prod_pool, b - 1, NK * len(POOL_N), last * len(POOL_N) + POOL_N.index(n) + 1)
                else:
                    reach(act, prod_vec, b - 1, NK * len(VEC_N), last * len(VEC_N) + VEC_N.index(n) + 1)
                nc.scalar.activation(Cc[:, n, :], W["B"][:, :], ACT.Copy).then_inc(C_ready, 1)

            def softplus(b, k):
                m = k + 1
                reach(act, v_done, b, NK, m)
                reach(act, dA_ready, b, UNITS, (k - 1) * NS)
                reach(act, dtu_ready, b, NK, k - 1)
                nc.scalar.activation(Dt[:, k % 2, :], W[BANK["v"]][:, :], ACT.Relu)
                reach(act, sp_sum, b, NK, m - 1)
                nc.scalar.activation(Sp_e[:, :], W[BANK["v"]][:, :], ACT.Abs).then_inc(sp_abs, 1)
                act.wait_ge(sp_abs, b.times(NK, m))
                nc.scalar.activation(Sp_e[:, :], Sp_e[:, :], ACT.Exp, scale=-1.0).then_inc(sp_e, 1)
                act.wait_ge(sp_e, b.times(NK, m))
                reach(act, sp_ln, b, NK, m - 1)
                nc.scalar.activation(Sp_1e[:, :], Sp_e[:, :], ACT.Identity, bias=1.0).then_inc(sp_1e, 1)

            def softplus_ln(b, k):
                act.wait_ge(sp_1e, b.times(NK, k + 1))
                reach(act, dt_ready, b, NK, k)
                nc.scalar.activation(Sp_ln[:, :], Sp_1e[:, :], ACT.Ln).then_inc(sp_ln, 1)

            def decay(b, k, n):
                unit = k * NS + n
                if n == 0:
                    reach(act, dt_ready, b, NK, k + 1)
                reach(act, h_ready, b, UNITS, unit - 1)
                nc.scalar.activation(dA[unit % 2][:, :], Dt[:, k % 2, :], ACT.Exp,
                                     scale=NegA[:, k, n:n + 1]).then_inc(dA_ready, 1)

            def z_tanh(b, k):
                reach(act, z_done, b, NK, k + 1)
                reach(act, gt_done, b, NK, k)
                nc.scalar.activation(G[:, :, :].rearrange("p t d -> p (t d)"), W[BANK["z"]][:, :], ACT.Tanh,
                                     scale=0.5).then_inc(tanh_z, 1)

            def gt_copy(b, k):
                reach(act, gt_done, b, NK, k + 1)
                if b.trip is None and b.const == 0 and k == 0:
                    act.wait_ge(ffn_ready, 1)
                if k < 2:
                    reach(act, nf_done, b, 2, 0)
                else:
                    reach(act, up_done, b, NC, ONE)
                    reach(act, gate_done, b, NC, ONE)
                nc.scalar.activation(Gt[:, k, :], W[BANK["gt"]][:, :], ACT.Copy, scale=0.5).then_inc(gt_copied, 1)

            def fg_tanh(b, half):
                reach(act, fg_done, b, 2, half + 1)
                reach(act, mixed, b, 2, 0)
                nc.scalar.activation(TanhF[:, 2 * half:2 * half + 2, :].rearrange("p t d -> p (t d)"),
                                     W[BANK["fg"][half]][:, :], ACT.Tanh, scale=0.5).then_inc(tanh_f, 1)

            def x1t_copy(b, c):
                reach(act, x1t_done, b, KM, c + 1)
                reach(act, nf_done, b, 2, 2)
                nc.scalar.activation(X1t[:, c, :], W[BANK["x1t"][c]][:, :], ACT.Copy).then_inc(x1t_copied, 1)

            def gate_tanh(b, c):
                reach(act, gate_done, b, NC, ONE + c + 1)
                reach(act, down_done, b, 2, ONE)
                nc.scalar.activation(Ht[:, c, :], W["A"][:, :], ACT.Tanh, scale=0.5).then_inc(tanh_g, 1)

            def iteration(b):
                post, scan, pre = has_post(b), has_scan(b), has_pre(b)
                for s in range(UNITS):
                    k, n = divmod(s, NS)
                    if scan:
                        decay(b, k, n)
                        if 0 <= s + UNITS - ACT_AT["bc"] < NS:
                            bc_copy(b, s + UNITS - ACT_AT["bc"])
                    if n == ACT_AT["gt"] and (scan if k else post):
                        gt_copy(*((b, k - 1) if k else (b - 1, NK - 1)))
                    if k < NK - 1 and scan:
                        if n == ACT_AT["sp"]:
                            softplus(b, k + 1)
                        if n == ACT_AT["ln"]:
                            softplus_ln(b, k + 1)
                    if n == ACT_AT["z"] and scan:
                        z_tanh(b, k)
                    if post:
                        for c in steps(ACT_AT, "x1t", s):
                            x1t_copy(b - 1, c)
                        for c in steps(ACT_AT, "gate", s):
                            gate_tanh(b - 1, c)
                    if scan:
                        for half in steps(ACT_AT, "fg", s):
                            fg_tanh(b, half)
                    if pre:
                        for j in steps(ACT_AT, "xi", s):
                            xi_copy(b + 1, j)
                        for j in steps(ACT_AT, "tanh", s):
                            xi_tanh(b + 1, j)
                        for part in steps(ACT_AT, "split", s):
                            split(b + 1, part)
                        if s == ACT_AT["sp0"]:
                            softplus(b + 1, 0)
                        if s == ACT_AT["ln0"]:
                            softplus_ln(b + 1, 0)
                        if 0 <= s - ACT_AT["bc"] < NS:
                            bc_copy(b + 1, s - ACT_AT["bc"])

            act.wait_ge(conv_ready, 1)
            iteration(Batch(-1))
            act.wait_ge(w_scan, 16 * LOADS["w_scan"])
            nc.scalar.activation(NegA[:, :, :], NegA[:, :, :], ACT.Exp).then_inc(a_exp, 1)
            act.wait_ge(a_ready, 1)
            batches(act, iteration)

        @block.gpsimd
        def _(pool):
            def log1p(b, k):
                reach(pool, sp_ln, b, NK, k + 1)
                pool.wait_ge(sp_gain, b.times(NK, k + 1))
                nc.gpsimd.tensor_tensor(Sp_ln[:, :], Sp_ln[:, :], Sp_e[:, :], ALU.subtract).then_inc(sp_sum, 1)

            def dt_u(b, k):
                reach(pool, dt_ready, b, NK, k + 1)
                reach(pool, u_ready, b, NK, NK)
                reach(pool, dBu_ready, b, UNITS, (k - 1) * NS)
                nc.gpsimd.tensor_tensor(DtU[:, k % 2, :], Dt[:, k % 2, :], U[:, b.parity, k, :],
                                        ALU.mult).then_inc(dtu_ready, 1)

            def drive(b, k, n):
                unit = k * NS + n
                if k == 0:
                    reach(pool, B_ready, b, NS, n + 1)
                if n == 0:
                    pool.wait_ge(dtu_ready, b.times(NK, k + 1))
                reach(pool, h_ready, b, UNITS, unit + 1 - DBU_RING)
                nc.gpsimd.tensor_tensor(DBu[:, unit % DBU_RING, :], DtU[:, k % 2, :], Bc[:, n, :],
                                        ALU.mult).then_inc(dBu_ready, 1)

            def product(b, k, n):
                unit = k * NS + n
                reach(pool, h_ready, b, UNITS, unit + 1)
                if k == 0:
                    reach(pool, C_ready, b, NS, n + 1)
                reach(pool, y_added, b, UNITS, unit + 1 - PROD_RING)
                nc.gpsimd.tensor_tensor(Prod[:, unit % PROD_RING, :], Hs[:, :], Cc[:, n, :],
                                        ALU.mult).then_inc(prod_pool, 1)

            def inverse_std(b, mv, Mv, var, Rs, rs, eps):
                reach(pool, mv, b, TB, TB)
                nc.gpsimd.tensor_tensor(Rs[:, :], Mv[:, :, 1], Eps[:, eps, :], ALU.add).then_inc(var, 1)
                pool.wait_ge(var, b.times(1, 1))
                nc.gpsimd.tensor_tensor(Rs[:, :], Rs[:, :], MinusHalf[:, :], ALU.pow).then_inc(rs, 1)

            def iteration(b):
                post, scan, pre = has_post(b), has_scan(b), has_pre(b)
                for s in range(UNITS):
                    k, n = divmod(s, NS)
                    if scan:
                        drive(b, k, n)
                        if n - 3 in POOL_N:
                            product(b, k, n - 3)
                    if k < NK - 1 and scan:
                        if n == POOL_AT["log"]:
                            log1p(b, k + 1)
                        if n == POOL_AT["dtu"]:
                            dt_u(b, k + 1)
                    if pre:
                        if s == POOL_AT["log0"]:
                            log1p(b + 1, 0)
                        if s == POOL_AT["dtu0"]:
                            dt_u(b + 1, 0)
                    if post:
                        if s == POOL_AT["rs1"]:
                            inverse_std(b - 1, mv1, Mv1, var1, Rs1, rs1, 1)
                        if s == POOL_AT["rs2"]:
                            inverse_std(b - 1, mv2, Mv2, var2, Rs2, rs2, 0)

            pool.wait_ge(const_ready, 1)
            iteration(Batch(-1))
            batches(pool, iteration)

        @block.vector
        def _(dve):
            def taps(b, j):
                reach(dve, xi_copied, b, NK, j + 1)
                for t in reversed(range(TAPS - 1)):
                    reach(dve, tap_done, b, NK * (TAPS - 1), j * (TAPS - 1) + TAPS - 2 - t)
                    c = U[:, b.parity, j, :]
                    ins = nc.vector.scalar_tensor_tensor(c, Xi[:, t:t + SEQ], ConvW[:, j, t:t + 1], c,
                                                         ALU.mult, ALU.add)
                    ins.then_inc(tap_done, 1)

            def u(b, j):
                reach(dve, tanh_c, b, NK, j + 1)
                c = U[:, b.parity, j, :]
                nc.vector.scalar_tensor_tensor(c, TanhC[:, :], 1.0, c, ALU.add, ALU.mult).then_inc(u_ready, 1)

            def split_rest(b, part):
                if part == 0:
                    reach(dve, split_hi, b, 1, 1)
                    nc.vector.tensor_tensor(Dbl[0:BC_PARTS, :], W[BANK["x_proj"]][0:BC_PARTS, :], DblS[:, :],
                                            ALU.subtract).then_inc(rest1, 1)
                else:
                    reach(dve, split_mid, b, 1, 1)
                    nc.vector.tensor_tensor(Dbl[64:96, :], Dbl[64:96, :], DblS[64:96, :],
                                            ALU.subtract).then_inc(rest2, 1)

            def rounding(b, k):
                reach(dve, sp_1e, b, NK, k + 1)
                nc.vector.scalar_tensor_tensor(Sp_e[:, :], Sp_1e[:, :], -1.0, Sp_e[:, :],
                                               ALU.add, ALU.subtract).then_inc(sp_gain, 1)

            def dt(b, k):
                reach(dve, sp_sum, b, NK, k + 1)
                nc.vector.tensor_tensor(Dt[:, k % 2, :], Sp_ln[:, :], Dt[:, k % 2, :], ALU.add).then_inc(dt_ready, 1)

            def scan_unit(b, k, n):
                unit = k * NS + n
                reach(dve, dA_ready, b, UNITS, unit + 1)
                reach(dve, dBu_ready, b, UNITS, unit + 1)
                if n in POOL_N:
                    reach(dve, prod_pool, b, NK * len(POOL_N), k * len(POOL_N) + POOL_N.index(n))
                    h = Hs
                else:
                    reach(dve, prod_vec, b, NK * len(VEC_N), vec_count(unit - 1))
                    h = H[unit % 2]
                nc.vector.tensor_tensor_scan(h[:, :], dA[unit % 2][:, :], DBu[:, unit % DBU_RING, :], 0.0,
                                             ALU.mult, ALU.add).then_inc(h_ready, 1)

            def product(b, k, n):
                unit = k * NS + n
                reach(dve, h_ready, b, UNITS, unit + 1)
                if k == 0:
                    reach(dve, C_ready, b, NS, n + 1)
                reach(dve, y_added, b, UNITS, unit + 1 - PROD_RING)
                nc.vector.tensor_tensor(Prod[:, unit % PROD_RING, :], H[unit % 2][:, :], Cc[:, n, :],
                                        ALU.mult).then_inc(prod_vec, 1)

            def z_silu(b, k):
                reach(dve, tanh_z, b, NK, k + 1)
                flat = G[:, :, :].rearrange("p t d -> p (t d)")
                nc.vector.scalar_tensor_tensor(flat, flat, 1.0, W[BANK["z"]][:, :], ALU.add, ALU.mult).then_inc(silu_z, 1)

            def gated(b, k):
                reach(dve, y_added, b, UNITS, (k + 1) * NS)
                dve.wait_ge(silu_z, b.times(NK, k + 1))
                flat = G[:, :, :].rearrange("p t d -> p (t d)")
                nc.vector.tensor_tensor(flat, Y[:, :], flat, ALU.mult).then_inc(g_ready, 1)

            def mix_terms(b, half):
                if half == 0:
                    dve.wait_ge(xn_loaded, b.times(16, 16))
                    reach(dve, stored, b, 16, ONE)
                rows = slice(2 * half, 2 * half + 2)
                reach(dve, tanh_f, b, 2, half + 1)
                nc.vector.scalar_tensor_tensor(X1[:, rows, :], TanhF[:, rows, :], 3.0, XN[:, rows, :],
                                               ALU.add, ALU.mult).then_inc(mix_parts, 1)
                reach(dve, nf_done, b, 2, half + 1)
                dve.wait_ge(mix_parts, b.times(4, 2 * half + 1))
                nc.vector.scalar_tensor_tensor(TanhF[:, rows, :], TanhF[:, rows, :], -1.0,
                                               W[BANK["nf"][half]][:, :].rearrange("p (t d) -> p t d", t=2),
                                               ALU.add, ALU.mult).then_inc(mix_parts, 1)

            def mix(b, half):
                rows = slice(2 * half, 2 * half + 2)
                dve.wait_ge(mix_parts, b.times(4, 2 * half + 2))
                nc.vector.tensor_tensor(X1[:, rows, :], X1[:, rows, :], TanhF[:, rows, :],
                                        ALU.subtract).then_inc(mixed, 1)
                statistics(b, half, mixed, Stats1, stats1)

            def statistics(b, half, source, Stats, stats):
                dve.wait_ge(source, b.times(2, half + 1))
                for t in (2 * half, 2 * half + 1):
                    nc.vector.bn_stats(Stats[:, t, :], X1[:, t, :]).then_inc(stats, 1)

            def aggregate(Stats, Mv, mv, half):
                for t in (2 * half, 2 * half + 1):
                    nc.vector.bn_aggr(Mv[:, t, :], Stats[:, t, :]).then_inc(mv, 1)

            def normalize(b, rs, Mv, Rs, ready):
                reach(dve, rs, b, 1, 1)
                for t in range(TB):
                    ins = nc.vector.tensor_scalar(X1[:, t, :], X1[:, t, :], Mv[:, t, 0:1], Rs[:, t:t + 1],
                                                  ALU.subtract, ALU.mult)
                ins.then_inc(ready, 1)

            def gate_silu(b, c):
                reach(dve, tanh_g, b, NC, c + 1)
                nc.vector.scalar_tensor_tensor(Ht[:, c, :], Ht[:, c, :], 1.0, W["A"][:, :],
                                               ALU.add, ALU.mult).then_inc(silu_g, 1)

            def gate_up(b, c):
                reach(dve, up_done, b, NC, ONE + c + 1)
                dve.wait_ge(silu_g, b.times(NC, c + 1))
                nc.vector.tensor_tensor(Ht[:, c, :], W["B"][:, :], Ht[:, c, :], ALU.mult).then_inc(hid_ready, 1)

            def residual(b, half):
                rows = slice(2 * half, 2 * half + 2)
                reach(dve, down_done, b, 2, ONE + half + 1)
                nc.vector.tensor_tensor(X1[:, rows, :], W[BANK["down"][half]][:, :].rearrange("p (t d) -> p t d", t=2),
                                        X1[:, rows, :], ALU.add).then_inc(summed, 1)
                statistics(b, half, summed, Stats2, stats2)

            def last_product(b):
                product(b, NK - 1, NS - 1)

            def iteration(b):
                post, scan, pre = has_post(b), has_scan(b), has_pre(b)
                for s in range(UNITS):
                    k, n = divmod(s, NS)
                    to_1 = [h for h in (0, 1) if post and s == DVE_AT["mix"][h] + 1]
                    to_2 = [h for h in (0, 1) if post and s == DVE_AT["sum"][h] + 1]
                    for h in to_1:
                        reach(dve, stats1, b - 1, TB, 2 * h + 2)
                    for h in to_2:
                        reach(dve, stats2, b - 1, TB, 2 * h + 2)
                    if scan:
                        scan_unit(b, k, n)
                    for h in to_1:
                        aggregate(Stats1, Mv1, mv1, h)
                    for h in to_2:
                        aggregate(Stats2, Mv2, mv2, h)
                    if s == 0 and post:
                        last_product(b - 1)
                    if scan and s and (s - 1) % NS not in POOL_N:
                        product(b, *divmod(s - 1, NS))
                    if n == DVE_AT["gated"] and (scan if k else post):
                        gated(*((b, k - 1) if k else (b - 1, NK - 1)))
                    if k < NK - 1 and scan:
                        if n == DVE_AT["round"]:
                            rounding(b, k + 1)
                        if n == DVE_AT["dt"]:
                            dt(b, k + 1)
                    if n == DVE_AT["z"] and scan:
                        z_silu(b, k)
                    if pre:
                        for j in steps(DVE_AT, "taps", s):
                            taps(b + 1, j)
                        for j in steps(DVE_AT, "u", s):
                            u(b + 1, j)
                        for part in steps(DVE_AT, "split", s):
                            split_rest(b + 1, part)
                        if s == DVE_AT["round0"]:
                            rounding(b + 1, 0)
                        if s == DVE_AT["dt0"]:
                            dt(b + 1, 0)
                    if post:
                        for half in steps(DVE_AT, "terms", s):
                            mix_terms(b - 1, half)
                        for half in steps(DVE_AT, "mix", s):
                            mix(b - 1, half)
                        if s == DVE_AT["x1"]:
                            normalize(b - 1, rs1, Mv1, Rs1, x1_ready)
                        for c in steps(DVE_AT, "gate", s):
                            gate_silu(b - 1, c)
                        for c in steps(DVE_AT, "up", s):
                            gate_up(b - 1, c)
                        for half in steps(DVE_AT, "sum", s):
                            residual(b - 1, half)
                        if s == DVE_AT["out"]:
                            normalize(b - 1, rs2, Mv2, Rs2, out_ready)

            def split_bias():
                rest, count = fgb_stage, 1
                for rows in (slice(0, 96), slice(32, 64), slice(64, 96), slice(64, 96)):
                    nc.vector.tensor_copy(FgS[rows, :], rest[rows, :]).then_inc(fgb_split, 1)
                    count += 1
                    dve.wait_ge(fgb_split, count)
                    if rows != slice(32, 64) and count < FGB_STEPS:
                        part = slice(0, 96) if rows == slice(0, 96) else slice(64, 96)
                        nc.vector.tensor_tensor(rest[part, :], rest[part, :], FgS[part, :],
                                                ALU.subtract).then_inc(fgb_split, 1)
                        count += 1
                        dve.wait_ge(fgb_split, count)
                assert count == FGB_STEPS

            nc.vector.memset(fgb_stage, 0.0).then_inc(fgb_split, 1)
            nc.vector.memset(Xi[:, 0:TAPS - 1], 0.0)
            nc.vector.memset(Ones[:, :], 1.0).then_inc(stored, ONE)
            nc.vector.memset(MinusHalf[:, :], -0.5).then_inc(down_done, ONE)
            nc.vector.memset(Eps[:, 0, :], EPS).then_inc(gate_done, ONE)
            nc.vector.memset(Eps[:, 1, :], 4 * EPS).then_inc(up_done, ONE)
            nc.vector.memset(Dbl[DT_ROW:P, :], 1.0)
            dve.wait_ge(w_in, 16 * LOADS["w_in"])
            nc.vector.tensor_scalar(ConvW[:, :, :], ConvW[:, :, :], 0.5, None, ALU.mult)
            nc.vector.tensor_scalar(ConvB[:, :], ConvB[:, :], 0.5, None, ALU.mult).then_inc(conv_ready, 1)
            dve.wait_ge(w_scan, 16 * LOADS["w_scan"])
            nc.vector.tensor_copy(Sel, Eye3[:, :].unsqueeze(2).broadcast_to([BC_PARTS, 2 * NS, P]))
            for k in range(NK):
                ins = nc.vector.tensor_scalar(DiagD[:, k, :], Id[:, :], Dcol[:, k:k + 1], None, ALU.mult)
            ins.then_inc(const_ready, 1)
            dve.wait_ge(conv_ready, 1)
            iteration(Batch(-1))
            dve.wait_ge(a_exp, 1)
            nc.vector.tensor_scalar(NegA[:, :, :], NegA[:, :, :], -1.0, None, ALU.mult).then_inc(a_ready, 1)
            dve.wait_ge(fgb_loaded, 16 * 6)
            split_bias()
            dve.wait_ge(w_post, 16 * LOADS["w_post"])
            nc.vector.tensor_scalar(Wgate[:, :, :].rearrange("p k n -> p (k n)"), gate_stage, DEQUANT, None, ALU.mult)
            nc.vector.tensor_scalar(Wup[:, :, :].rearrange("p k n -> p (k n)"), up_stage, DEQUANT, None, ALU.mult)
            nc.vector.tensor_scalar(Wdown[:, :, :].rearrange("p k n -> p (k n)"), down_stage, DEQUANT, 0.5,
                                    ALU.mult, ALU.mult).then_inc(ffn_ready, 1)
            batches(dve, iteration)


BANK = {
    "xi": "ABAB", "x_proj": "C", "v": "C", "z": "C", "fg": "AB", "gt": "C", "nf": "AB", "x1t": "CA", "down": "CC",
}

PE_AT = {
    "open": 1, "gt": 1, "v": 3, "v0": 50, "z": 10, "nf": (3, 4, 6, 8), "xi": (9, 11, 12, 19), "x1t": (15, 16),
    "gate": (22, 25, 30, 34, 40, 42), "up": (24, 29, 32, 36, 41, 44), "x_proj": 36, "fg": (46, 47),
    "down": (52, 52, 53, 55), "bc": 48,
}
ACT_AT = {
    "gt": 6, "sp": 8, "ln": 10, "sp0": 56, "ln0": 58, "z": 15, "xi": (13, 16, 18, 23), "tanh": (17, 19, 25, 27),
    "x1t": (20, 22), "gate": (27, 31, 36, 39, 43, 47), "split": (42, 45, 49), "fg": (50, 52), "bc": 53,
}
DVE_AT = {
    "gated": 1, "round": 8, "dt": 10, "round0": 54, "dt0": 57, "z": 14, "terms": (8, 11), "mix": (9, 12), "x1": 15,
    "taps": (13, 16, 21, 23), "u": (17, 19, 25, 30), "gate": (26, 30, 34, 38, 43, 46),
    "up": (26, 32, 36, 39, 43, 48), "split": (41, 48), "sum": (56, 60), "out": 63,
}
POOL_AT = {
    "log": 11, "dtu": 15, "log0": 58, "dtu0": 62, "rs1": 17, "rs2": 62,
}

LOADS = {"w_in": 3, "w_scan": 11, "w_post": 5}


FGB_STEPS = 7


def steps(at, name, s):
    return [i for i, slot in enumerate(at[name]) if slot == s]


def vec_count(units):
    whole, part = divmod(units, NS)
    return whole * len(VEC_N) + sum(n < part for n in VEC_N)


def kernel(**inputs):
    import numpy as np
    import concourse.bacc as bacc
    from concourse.bass_utils import run_bass_kernel_spmd

    a = {n.replace("L0_attn_", "").replace("L0_ffn_", ""): np.asarray(v) for n, v in inputs.items()}
    eye = np.eye(P, dtype=np.float32)
    eye_bc = np.eye(2 * NS, dtype=np.float32)
    arrays = {
        "x": a["x"].reshape(BATCH * SEQ, DM),
        "xT": a["x"].transpose(0, 2, 1).reshape(BATCH * DM, SEQ),
        "in_w": a["in_proj_w"],
        "conv_w": a["conv_w"],
        "conv_b": a["conv_b"].reshape(NK, P).T,
        "xp_w": a["x_proj_w"],
        "dt_w": a["dt_proj_w"],
        "dt_b": a["dt_proj_b"],
        "a_log": a["A_log"],
        "d_skip": a["D"].reshape(NK, P).T,
        "out_w": a["out_proj_w"],
        "fg_w": a["fg_w"],
        "fg_b": a["fg_b"],
        "gate_wT": a["w_gate"].T,
        "up_wT": a["w_up"].T,
        "down_wT": a["w_down"].T,
        "ident": eye,
        "eye3": np.concatenate([eye_bc, eye_bc, eye_bc]),
    }
    nc = bacc.Bacc("TRN2", target_bir_lowering=False, num_devices=1)
    args = {}
    for name, v in arrays.items():
        arrays[name] = np.ascontiguousarray(v)
        args[name] = nc.dram_tensor(f"in_{name}", v.shape, mybir.dt.from_np(v.dtype), kind="ExternalInput").ap()
    out = nc.dram_tensor("out_dram", (BATCH * SEQ, DM), F32, kind="ExternalOutput").ap()
    build(nc, *args.values(), out)
    r = run_bass_kernel_spmd(nc, [{f"in_{n}": v for n, v in arrays.items()}], core_ids=[0])
    return r.results[0]["out_dram"].reshape(BATCH, SEQ, DM)
```

```python
from contextlib import ExitStack

import concourse.bass as bass
from concourse import mybir

F32 = mybir.dt.float32
BF16 = mybir.dt.bfloat16
I32 = mybir.dt.int32
ALU = mybir.AluOpType
ACT = mybir.ActivationFunctionType

BATCH, SEQ, DM = 8, 512, 256
DI, NS, TAPS, RANK = 512, 16, 4, 16
HID = 768
P = 128
NK = DI // P
KM = DM // P
TB = SEQ // P
NC = HID // P
UNITS = NK * NS
EPS = 1e-5
DEQUANT = 1.0 / 127.0

POOL_UNITS = (
    7, 10, 14, 15, 24, 29, 34, 38, 59,
)
DA_RING, DBU_RING, PROD_RING = 4, 4, 4
POOL_LAG = 3
ONE = 1
BC_PARTS = 96
DT_ROW = 96

TRIPS = (BATCH - 2) // 2


class Batch:

    def __init__(self, const, trip=None):
        self.const, self.trip = const, trip

    def __add__(self, d):
        return Batch(self.const + d, self.trip)

    def __sub__(self, d):
        return Batch(self.const - d, self.trip)

    @property
    def parity(self):
        return self.const % 2

    def times(self, per, extra=0):
        if self.trip is None:
            return per * self.const + extra
        return self.trip * (2 * per) + (per * self.const + extra)


def reach(eng, sem, b, per, extra):
    if per * b.const + extra <= 0:
        assert b.trip is None
        return
    eng.wait_ge(sem, b.times(per, extra))


def batches(eng, iteration):
    iteration(Batch(0))
    with eng.Fori(0, TRIPS) as trip:
        for c in (1, 2):
            iteration(Batch(c, trip))
    for c in (BATCH - 1, BATCH):
        iteration(Batch(c))


def first(b):
    return b.trip is None and b.const == 0


def has_post(b):
    return b.trip is not None or b.const >= 1


def has_scan(b):
    return b.trip is not None or 0 <= b.const < BATCH


def has_pre(b):
    return b.trip is not None or b.const < BATCH - 1


def opening(b, name, at, s, step, early=2):
    for k in steps(at, name, s):
        if k >= early and has_scan(b):
            step(b, k)
        elif k < early and has_pre(b):
            step(b + 1, k)


def closing(b, name, at, s, step):
    for k in steps(at, name, s):
        if k < NK - 1 and has_scan(b):
            step(b, k)
        elif k == NK - 1 and has_post(b):
            step(b - 1, k)


def spread_now(b, at, s):
    if first(b):
        return [s + at["ahead"]] if s + at["ahead"] < NS else []
    return steps(at, "bc", UNITS + s) if has_scan(b) else []


def build(nc, x, xT, in_w, conv_w, conv_b, xp_w, dt_w, dt_b, a_log, d_skip, out_w, fg_w, fg_b,
          gate_wT, up_wT, down_wT, ident, eye3, out):
    ctx = ExitStack()
    with ctx:
        def sb(name, shape, dt=F32):
            return ctx.enter_context(nc.sbuf_tensor(name, shape, dt))

        def ps(name):
            return ctx.enter_context(nc.psum_tensor(name, [P, SEQ], F32))

        def sem(name):
            return ctx.enter_context(nc.semaphore(name))

        Win = sb("Win", [P, KM, 2 * DI])
        Wxp = sb("Wxp", [P, NK, BC_PARTS + RANK])
        Wout = sb("Wout", [P, NK, DM])
        Wfg = sb("Wfg", [P, KM, DM])
        FgS = sb("FgS", [BC_PARTS, 2 * DM], BF16)
        Wgate = sb("Wgate", [P, KM, HID])
        Wup = sb("Wup", [P, KM, HID])
        Wdown = sb("Wdown", [P, NC, DM])
        Id = sb("Id", [P, P])
        Eye3 = sb("Eye3", [BC_PARTS, 2 * NS])
        SelDt = sb("SelDt", [P, 2 * NS, P], BF16)
        Sel = SelDt[0:BC_PARTS, :, :]
        Wdt = SelDt[:, 0:2 * DI // P, :].rearrange("p r c -> p (r c)").bitcast(F32)
        DiagD = sb("DiagD", [P, NK, P])
        ConvW = sb("ConvW", [P, NK, TAPS])
        ConvB = sb("ConvB", [P, NK])
        Dcol = sb("Dcol", [P, NK])
        NegA = sb("NegA", [P, NK, NS])
        Ones = sb("Ones", [BC_PARTS, P], BF16)
        MinusHalf = sb("MinusHalf", [P, TB])
        Eps = sb("Eps", [P, 2, TB])

        XT = sb("XT", [P, 2, KM, SEQ])
        Bc = sb("Bc", [P, NS, SEQ])
        Cc = sb("Cc", [P, NS, SEQ])
        Xi = sb("Xi", [P, TAPS - 1 + SEQ])
        U = sb("U", [P, 2, NK, SEQ])
        TanhC = sb("TanhC", [P, SEQ])
        DblS = sb("DblS", [BC_PARTS, SEQ], BF16)
        Dbl = sb("Dbl", [P, SEQ])
        Sp_e = sb("Sp_e", [P, 2, SEQ])
        Sp_1e = sb("Sp_1e", [P, 2, SEQ])
        Dt = sb("Dt", [P, NK, SEQ])
        DtU = sb("DtU", [P, 2, SEQ])
        DBu = sb("DBu", [P, DBU_RING, SEQ])
        Prod = sb("Prod", [P, PROD_RING, SEQ])
        G = sb("G", [P, TB, P])
        Gt = sb("Gt", [P, NK, SEQ])
        TanhF = sb("TanhF", [P, TB, DM])
        X1 = sb("X1", [P, TB, DM])
        Ht = sb("Ht", [P, NC, SEQ])
        Stats1 = sb("Stats1", [P, TB, 6])
        Mv1 = sb("Mv1", [P, TB, 2])
        Rs1 = sb("Rs1", [P, TB])
        Stats2 = sb("Stats2", [P, TB, 6])
        Mv2 = sb("Mv2", [P, TB, 2])
        Rs2 = sb("Rs2", [P, TB])
        X1t = Gt[:, 2:4, :]
        FirstXi = Cc[:, 0:5, :].rearrange("p n t -> p (n t)")[:, 0:NK * (TAPS - 1 + SEQ)].rearrange(
            "p (k t) -> p k t", k=NK)
        FirstTanh = Cc[:, NS - NK:NS, :]

        def xi_tile(b, j):
            return FirstXi[:, j, :] if first(b) else Xi

        def tanh_tile(b, j):
            return FirstTanh[:, j, :] if first(b) else TanhC[:, :]

        dA = [ps(f"dA{i}") for i in range(DA_RING)]
        Y = ps("Y")
        W = {name: ps(f"work{name}") for name in "ABC"}

        w_in = sem("w_in")
        w_const = sem("w_const")
        w_scan = sem("w_scan")
        w_post = sem("w_post")
        xt_loaded = [sem(f"xt_loaded{i}") for i in range(2)]
        xn_loaded = sem("xn_loaded")
        stored = sem("stored")
        conv_ready = sem("conv_ready")
        const_ready = sem("const_ready")
        ffn_ready = sem("ffn_ready")
        fgb_loaded = sem("fgb_loaded")
        fgb_split = sem("fgb_split")
        a_exp = sem("a_exp")
        a_ready = sem("a_ready")
        xi_done = sem("xi_done")
        xi_copied = sem("xi_copied")
        tap_done = sem("tap_done")
        tanh_c = sem("tanh_c")
        u_ready = sem("u_ready")
        dbl_done = sem("dbl_done")
        split_hi = sem("split_hi")
        rest1 = sem("rest1")
        split_mid = sem("split_mid")
        rest2 = sem("rest2")
        split_lo = sem("split_lo")
        bcB_done, bcC_done = sem("bcB_done"), sem("bcC_done")
        B_ready, C_ready = sem("B_ready"), sem("C_ready")
        v_done = sem("v_done")
        sp_abs = sem("sp_abs")
        sp_e = sem("sp_e")
        sp_1e = sem("sp_1e")
        sp_ln = sem("sp_ln")
        sp_gain = sem("sp_gain")
        sp_sum = sem("sp_sum")
        dt_ready = sem("dt_ready")
        dtu_ready = sem("dtu_ready")
        dA_ready = sem("dA_ready")
        dBu_ready = sem("dBu_ready")
        h_ready = sem("h_ready")
        prod_vec = sem("prod_vec")
        prod_pool = sem("prod_pool")
        y_added = sem("y_added")
        z_done = sem("z_done")
        tanh_z = sem("tanh_z")
        silu_z = sem("silu_z")
        g_ready = sem("g_ready")
        gt_done = sem("gt_done")
        gt_copied = sem("gt_copied")
        fg_done = sem("fg_done")
        tanh_f = sem("tanh_f")
        nf_done = sem("nf_done")
        mix_parts = sem("mix_parts")
        mixed = sem("mixed")
        stats1 = sem("stats1")
        mv1 = sem("mv1")
        var1 = sem("var1")
        rs1 = sem("rs1")
        x1_ready = sem("x1_ready")
        x1t_done = sem("x1t_done")
        x1t_copied = sem("x1t_copied")
        gate_done, up_done = sem("gate_done"), sem("up_done")
        tanh_g = sem("tanh_g")
        silu_g = sem("silu_g")
        hid_ready = sem("hid_ready")
        down_done = sem("down_done")
        summed = sem("summed")
        stats2 = sem("stats2")
        mv2 = sem("mv2")
        var2 = sem("var2")
        rs2 = sem("rs2")
        out_ready = sem("out_ready")

        gate_stage = Ht[:, 0:3, :].rearrange("p a b -> p (a b)").bitcast(I32)
        up_stage = Ht[:, 3:6, :].rearrange("p a b -> p (a b)").bitcast(I32)
        down_stage = Gt[:, 0:3, :].rearrange("p a b -> p (a b)").bitcast(I32)

        fgb_stage = TanhF[0:BC_PARTS, 0:2, :].rearrange("p t d -> p (t d)")

        block = ctx.enter_context(nc.Block())

        @block.sync
        def _(sp):
            def rows(dram, b, count):
                if b.trip is None:
                    return dram[b.times(count):b.times(count) + count, :]
                return dram[bass.ds(sp.snap(b.times(count)), count), :]

            bc_w = xp_w[:, RANK:RANK + 2 * NS].rearrange("(k p) n -> p k n", p=P)
            loads = {
                w_in: [
                    (Win[:, :, 0:DI], in_w[:, 0:DI].rearrange("(k p) n -> p k n", p=P)),
                    (ConvW[:, :, :], conv_w.rearrange("(k p) o t -> p k (o t)", p=P)),
                    (ConvB[:, :], conv_b),
                ],
                w_scan: [
                    (Wxp[:, :, 0:32], bc_w), (Wxp[:, :, 32:64], bc_w), (Wxp[:, :, 64:96], bc_w),
                    (Wxp[:, :, 96:96 + RANK], xp_w[:, 0:RANK].rearrange("(k p) n -> p k n", p=P)),
                    (Wdt[DT_ROW:DT_ROW + RANK, :], dt_w),
                    (Wdt[DT_ROW + RANK:DT_ROW + RANK + 1, :], dt_b.rearrange("(o n) -> o n", o=1)),
                    (NegA[:, :, :], a_log.rearrange("(k p) n -> p k n", p=P)),
                    (Win[:, :, DI:], in_w[:, DI:].rearrange("(k p) n -> p k n", p=P)),
                ],
                w_post: [
                    (Wfg[:, :, :], fg_w.rearrange("(k p) n -> p k n", p=P)),
                    (Wout[:, :, :], out_w.rearrange("(k p) n -> p k n", p=P)),
                    (gate_stage.rearrange("p (k n) -> p k n", k=KM), gate_wT.rearrange("(k p) n -> p k n", p=P)),
                    (up_stage.rearrange("p (k n) -> p k n", k=KM), up_wT.rearrange("(k p) n -> p k n", p=P)),
                    (down_stage.rearrange("p (k n) -> p k n", k=NC), down_wT.rearrange("(k p) n -> p k n", p=P)),
                ],
            }

            def load_xt(b, source):
                sp.dma_start(XT[:, b.parity, :, :], source.rearrange("(k p) t -> p k t", p=P)
                             ).then_inc(xt_loaded[b.parity], 16)

            load_xt(Batch(0), rows(xT, Batch(0), KM * P))
            for loaded, parts in loads.items():
                assert len(parts) == LOADS[loaded.name]
                for dst, src in parts:
                    sp.dma_start(dst, src).then_inc(loaded, 16)

            def iteration(b):
                if has_scan(b) and has_pre(b):
                    source = rows(xT, b + 1, KM * P)
                    reach(sp, z_done, b - 1, NK, NK)
                    load_xt(b + 1, source)
                if has_post(b):
                    target = rows(out, b - 1, SEQ)
                    reach(sp, out_ready, b - 1, 1, 1)
                    sp.dma_start(target.rearrange("(t p) d -> p t d", p=P), X1[:, :, :]).then_inc(stored, 16)
                if has_scan(b):
                    source = rows(x, b, SEQ)
                    reach(sp, stored, b, 16, ONE)
                    sp.dma_start(X1[:, :, :], source.rearrange("(t p) d -> p t d", p=P)).then_inc(xn_loaded, 16)

            sp.wait_ge(fgb_split, 1)
            for row in (0, 32, 64):
                for half in (0, 1):
                    sp.dma_start(fgb_stage[row:row + 1, half * DM:(half + 1) * DM],
                                 fg_b.rearrange("(o n) -> o n", o=1)).then_inc(fgb_loaded, 16)
            batches(sp, iteration)
            sp.wait_ge(stored, 16 * BATCH + ONE)

        @block.tensor
        def _(pe):
            read_by = {name: None for name in W}

            def take(name, sem, b, per, extra):
                if read_by[name]:
                    before, when, *count = read_by[name]
                    pe.wait_ge(before, when.times(*count))
                read_by[name] = (sem, b, per, extra)
                return W[name]

            def xi(b, j):
                if j == 0:
                    before = 16 * (b.const // 2)
                    pe.wait_ge(xt_loaded[b.parity], before + 16 if b.trip is None else b.trip * 16 + (before + 16))
                bank = take(BANK["xi"][j], xi_copied, b, NK, j + 1)
                for k in range(KM):
                    mm = nc.tensor.matmul(bank[:, :], Win[:, k, j * P:(j + 1) * P], XT[:, b.parity, k, :],
                                          start=(k == 0), stop=(k == KM - 1))
                mm.then_inc(xi_done, 1)

            def x_proj(b):
                if first(b):
                    pe.wait_ge(w_scan, 16 * LOADS["w_scan"])
                    pe.wait_ge(const_ready, 1)
                bank = take(BANK["x_proj"], rest1, b, 1, 1)
                for k in range(NK):
                    reach(pe, u_ready, b, NK, k + 1)
                    mm = nc.tensor.matmul(bank[0:BC_PARTS + RANK, :], Wxp[:, k, :], U[:, b.parity, k, :],
                                          start=(k == 0), stop=(k == NK - 1))
                mm.then_inc(dbl_done, 1)

            def broadcast(b, n):
                if n == 0:
                    reach(pe, split_lo, b, 1, 1)
                for name, row, done, ready in (("A", n, bcB_done, B_ready), ("B", NS + n, bcC_done, C_ready)):
                    bank = take(name, ready, b, NS, n + 1)
                    nc.tensor.matmul(bank[:, :], Sel[:, row, :], DblS[:, :], start=True, stop=True).then_inc(done, 1)

            def dt_arg(b, k):
                bank = take(BANK["v"][k], sp_abs, b, NK, k + 1)
                if k == 0:
                    reach(pe, split_hi, b, 1, 1)
                rows = slice(DT_ROW, DT_ROW + RANK + 1)
                nc.tensor.matmul(bank[:, :], Wdt[rows, k * P:(k + 1) * P], Dbl[rows, :],
                                 start=True, stop=True).then_inc(v_done, 1)

            def z(b, k):
                bank = take(BANK["z"][k], silu_z, b, NK, k + 1)
                for t in range(TB):
                    for c in range(KM):
                        mm = nc.tensor.matmul(bank[:, t * P:(t + 1) * P], XT[:, b.parity, c, t * P:(t + 1) * P],
                                              Win[:, c, DI + k * P:DI + (k + 1) * P],
                                              start=(c == 0), stop=(c == KM - 1))
                mm.then_inc(z_done, 1)

            def feature_gate(b, half):
                if first(b) and half == 0:
                    pe.wait_ge(fgb_split, FGB_STEPS)
                bank = take(BANK["fg"][half], tanh_f, b, 2, half + 1)
                nc.tensor.matmul(bank[:, :], Ones[:, :], FgS[:, :], start=True, stop=False, skip_group_check=True)
                for t in range(2):
                    rows = slice((2 * half + t) * P, (2 * half + t + 1) * P)
                    for c in range(KM):
                        mm = nc.tensor.matmul(bank[:, t * DM:(t + 1) * DM], XT[:, b.parity, c, rows], Wfg[:, c, :],
                                              start=False, stop=(c == KM - 1), skip_group_check=True)
                mm.then_inc(fg_done, 1)

            def y_skip(b, k):
                if k or has_post(b):
                    reach(pe, g_ready, b, NK, k)
                for t in range(TB):
                    nc.tensor.matmul(Y[:, t * P:(t + 1) * P], U[:, b.parity, k, t * P:(t + 1) * P], DiagD[:, k, :],
                                     start=(t == 0), stop=False, skip_group_check=True)

            def y_add(b, k, n):
                unit = k * NS + n
                reach_product(pe, prod_vec, prod_pool, b, unit)
                slot = unit % PROD_RING
                for t in range(TB):
                    mm = nc.tensor.matmul(Y[:, t * P:(t + 1) * P], Prod[:, slot, t * P:(t + 1) * P], Id[:, :],
                                          start=False, stop=(n == NS - 1), is_transpose=True,
                                          skip_group_check=True)
                mm.then_inc(y_added, 1)

            def g_transpose(b, k):
                bank = take(BANK["gt"][k], gt_copied, b, NK, k + 1)
                reach(pe, g_ready, b, NK, k + 1)
                for t in range(TB):
                    mm = nc.tensor.transpose(bank[:, t * P:(t + 1) * P], G[:, t, :], Id[:, :])
                mm.then_inc(gt_done, 1)

            def out_proj(b, t):
                if t == 0:
                    reach(pe, gt_copied, b, NK, NK)
                if t % 2 == 0:
                    take(BANK["nf"][t // 2], mix_parts, b, 4, t + 2)
                for c in range(NK):
                    mm = nc.tensor.matmul(W[BANK["nf"][t // 2]][:, (t % 2) * DM:(t % 2 + 1) * DM], Gt[:, c, t * P:(t + 1) * P],
                                          Wout[:, c, :], start=(c == 0), stop=(c == NK - 1))
                if t % 2:
                    mm.then_inc(nf_done, 1)

            def x1_transpose(b, c):
                bank = take(BANK["x1t"][c], x1t_copied, b, KM, c + 1)
                if c == 0:
                    reach(pe, x1_ready, b, 1, 1)
                for t in range(TB):
                    mm = nc.tensor.transpose(bank[:, t * P:(t + 1) * P], X1[:, t, c * P:(c + 1) * P], Id[:, :])
                mm.then_inc(x1t_done, 1)

            def hidden(b, c, name, weights, done, read):
                bank = take(name, read, b, NC, c + 1)
                if c == 0:
                    reach(pe, x1t_copied, b, KM, KM)
                for k in range(KM):
                    mm = nc.tensor.matmul(bank[:, :], weights[:, k, c * P:(c + 1) * P], X1t[:, k, :],
                                          start=(k == 0), stop=(k == KM - 1))
                mm.then_inc(done, 1)

            def down(b, t):
                if t == 0:
                    reach(pe, hid_ready, b, NC, NC)
                if t % 2 == 0:
                    take(BANK["down"][t // 2], summed, b, 2, t // 2 + 1)
                for c in range(NC):
                    mm = nc.tensor.matmul(W[BANK["down"][t // 2]][:, (t % 2) * DM:(t % 2 + 1) * DM], Ht[:, c, t * P:(t + 1) * P],
                                          Wdown[:, c, :], start=(c == 0), stop=(c == NC - 1))
                if t % 2:
                    mm.then_inc(down_done, 1)

            def iteration(b):
                post, scan, pre = has_post(b), has_scan(b), has_pre(b)
                for s in range(UNITS):
                    k, n = divmod(s, NS)
                    if scan and s == PE_AT["open"][k]:
                        y_skip(b, k)
                        for first in range(n):
                            y_add(b, k, first)
                    if scan and s >= PE_AT["open"][k]:
                        y_add(b, k, n)
                    for m in spread_now(b, PE_AT, s):
                        broadcast(b, m)
                    closing(b, "gt", PE_AT, s, g_transpose)
                    opening(b, "v", PE_AT, s, dt_arg)
                    if scan:
                        for g in steps(PE_AT, "z", s):
                            z(b, g)
                    if post:
                        for t in steps(PE_AT, "nf", s):
                            out_proj(b - 1, t)
                        for c in steps(PE_AT, "x1t", s):
                            x1_transpose(b - 1, c)
                        for c in steps(PE_AT, "gate", s):
                            hidden(b - 1, c, BANK["gate"][c], Wgate, gate_done, silu_g)
                        for c in steps(PE_AT, "up", s):
                            hidden(b - 1, c, BANK["up"][c], Wup, up_done, hid_ready)
                        for t in steps(PE_AT, "down", s):
                            down(b - 1, t)
                    if scan:
                        for half in steps(PE_AT, "fg", s):
                            feature_gate(b, half)
                    if pre:
                        for c in steps(PE_AT, "xi", s):
                            xi(b + 1, c)
                        if s == PE_AT["x_proj"]:
                            x_proj(b + 1)
                        for m in steps(PE_AT, "bc", s):
                            broadcast(b + 1, m)

            b = Batch(0)
            pe.wait_ge(w_in, 16 * LOADS["w_in"])
            for j in range(NK):
                xi(b, j)
            x_proj(b)
            dt_arg(b, 0)
            dt_arg(b, 1)
            for n in range(PE_AT["ahead"]):
                broadcast(b, n)
            pe.wait_ge(w_post, 16 * LOADS["w_post"])
            iteration(Batch(0))
            pe.wait_ge(ffn_ready, 1)
            with pe.Fori(0, TRIPS) as trip:
                for name, (sem_, b, *count) in read_by.items():
                    read_by[name] = (sem_, Batch(b.const, trip), *count)
                for c in (1, 2):
                    iteration(Batch(c, trip))
            for name, (sem_, b, *count) in read_by.items():
                read_by[name] = (sem_, Batch(b.const + 2 * (TRIPS - 1)), *count)
            for c in (BATCH - 1, BATCH):
                iteration(Batch(c))

        @block.scalar
        def _(act):
            def xi_copy(b, j):
                reach(act, xi_done, b, NK, j + 1)
                if not first(b):
                    reach(act, tap_done, b, NK * (TAPS - 1), j * (TAPS - 1))
                reach(act, y_added, b - 2, UNITS, UNITS)
                reach(act, dtu_ready, b - 2, NK, NK)
                bank = W[BANK["xi"][j]]
                nc.scalar.activation(xi_tile(b, j)[:, TAPS - 1:], bank[:, :], ACT.Copy)
                nc.scalar.activation(U[:, b.parity, j, :], bank[:, :], ACT.Identity, bias=ConvB[:, j:j + 1],
                                     scale=ConvW[:, j, TAPS - 1:TAPS]).then_inc(xi_copied, 1)

            def xi_tanh(b, j):
                reach(act, tap_done, b, NK * (TAPS - 1), (j + 1) * (TAPS - 1))
                if not first(b):
                    reach(act, u_ready, b, NK, j)
                nc.scalar.activation(tanh_tile(b, j), U[:, b.parity, j, :], ACT.Tanh).then_inc(tanh_c, 1)

            def split(b, part):
                if part == 0:
                    reach(act, dbl_done, b, 1, 1)
                    reach(act, bcC_done, b, NS, 0)
                    reach(act, v_done, b, NK, 0)
                    reach(act, split_lo, b, 1, 0)
                    rows = slice(DT_ROW, DT_ROW + RANK)
                    nc.scalar.activation(Dbl[rows, :], W[BANK["x_proj"]][rows, :], ACT.Copy)
                    nc.scalar.activation(DblS[:, :], W[BANK["x_proj"]][0:BC_PARTS, :], ACT.Copy).then_inc(split_hi, 1)
                elif part == 1:
                    reach(act, rest1, b, 1, 1)
                    nc.scalar.activation(DblS[32:64, :], Dbl[32:64, :], ACT.Copy)
                    nc.scalar.activation(DblS[64:96, :], Dbl[64:96, :], ACT.Copy).then_inc(split_mid, 1)
                else:
                    reach(act, rest2, b, 1, 1)
                    nc.scalar.activation(DblS[64:96, :], Dbl[64:96, :], ACT.Copy).then_inc(split_lo, 1)

            def bc_copy(b, n):
                last = NK - 1
                reach(act, bcB_done, b, NS, n + 1)
                reach(act, dBu_ready, b - 1, UNITS, last * NS + n + 1)
                nc.scalar.activation(Bc[:, n, :], W["A"][:, :], ACT.Copy).then_inc(B_ready, 1)
                reach(act, bcC_done, b, NS, n + 1)
                reach_product(act, prod_vec, prod_pool, b - 1, last * NS + n)
                nc.scalar.activation(Cc[:, n, :], W["B"][:, :], ACT.Copy).then_inc(C_ready, 1)

            def softplus_abs(b, k):
                reach(act, v_done, b, NK, k + 1)
                reach(act, dA_ready, b - 1, UNITS, (k + 1) * NS)
                reach(act, dtu_ready, b - 1, NK, k + 1)
                nc.scalar.activation(Dt[:, k, :], W[BANK["v"][k]][:, :], ACT.Relu)
                reach(act, sp_sum, b, NK, k - 1)
                nc.scalar.activation(Sp_e[:, k % 2, :], W[BANK["v"][k]][:, :], ACT.Abs).then_inc(sp_abs, 1)

            def softplus_e(b, k):
                act.wait_ge(sp_abs, b.times(NK, k + 1))
                nc.scalar.activation(Sp_e[:, k % 2, :], Sp_e[:, k % 2, :], ACT.Exp, scale=-1.0).then_inc(sp_e, 1)

            def softplus_1e(b, k):
                act.wait_ge(sp_e, b.times(NK, k + 1))
                reach(act, dt_ready, b, NK, k - 1)
                nc.scalar.activation(Sp_1e[:, k % 2, :], Sp_e[:, k % 2, :], ACT.Identity, bias=1.0).then_inc(sp_1e, 1)

            def softplus_ln(b, k):
                reach(act, sp_gain, b, NK, k + 1)
                act.wait_ge(sp_1e, b.times(NK, k + 1))
                nc.scalar.activation(Sp_1e[:, k % 2, :], Sp_1e[:, k % 2, :], ACT.Ln).then_inc(sp_ln, 1)

            def decay(b, k, n):
                unit = k * NS + n
                if n == 0:
                    reach(act, dt_ready, b, NK, k + 1)
                before, last = (b, unit - DA_RING) if unit >= DA_RING else (b - 1, unit - DA_RING + UNITS)
                if last in POOL_UNITS:
                    reach(act, h_ready, before, UNITS, last + 1)
                else:
                    reach_product(act, prod_vec, prod_pool, before, last)
                nc.scalar.activation(dA[unit % DA_RING][:, :], Dt[:, k, :], ACT.Exp,
                                     scale=NegA[:, k, n:n + 1]).then_inc(dA_ready, 1)

            def z_tanh(b, k):
                reach(act, z_done, b, NK, k + 1)
                reach(act, gt_done, b, NK, k)
                nc.scalar.activation(G[:, :, :].rearrange("p t d -> p (t d)"), W[BANK["z"][k]][:, :], ACT.Tanh,
                                     scale=0.5).then_inc(tanh_z, 1)

            def gt_copy(b, k):
                reach(act, gt_done, b, NK, k + 1)
                if first(b) and k == 0:
                    act.wait_ge(ffn_ready, 1)
                if k < 2:
                    reach(act, nf_done, b, 2, 0)
                else:
                    reach(act, up_done, b, NC, ONE)
                    reach(act, gate_done, b, NC, ONE)
                nc.scalar.activation(Gt[:, k, :], W[BANK["gt"][k]][:, :], ACT.Copy, scale=0.5).then_inc(gt_copied, 1)

            def fg_tanh(b, half):
                reach(act, fg_done, b, 2, half + 1)
                reach(act, mixed, b, 2, 0)
                nc.scalar.activation(TanhF[:, 2 * half:2 * half + 2, :].rearrange("p t d -> p (t d)"),
                                     W[BANK["fg"][half]][:, :], ACT.Tanh, scale=0.5).then_inc(tanh_f, 1)

            def x1t_copy(b, c):
                reach(act, x1t_done, b, KM, c + 1)
                reach(act, nf_done, b, 2, 2)
                nc.scalar.activation(X1t[:, c, :], W[BANK["x1t"][c]][:, :], ACT.Copy).then_inc(x1t_copied, 1)

            def gate_tanh(b, c):
                reach(act, gate_done, b, NC, ONE + c + 1)
                reach(act, down_done, b, 2, ONE)
                nc.scalar.activation(Ht[:, c, :], W[BANK["gate"][c]][:, :], ACT.Tanh, scale=0.5).then_inc(tanh_g, 1)

            def iteration(b):
                post, scan, pre = has_post(b), has_scan(b), has_pre(b)
                for s in range(UNITS):
                    k, n = divmod(s, NS)
                    if scan:
                        decay(b, k, n)
                        for m in spread_now(b, ACT_AT, s):
                            bc_copy(b, m)
                    closing(b, "gt", ACT_AT, s, gt_copy)
                    opening(b, "abs", ACT_AT, s, softplus_abs)
                    opening(b, "e", ACT_AT, s, softplus_e)
                    opening(b, "1e", ACT_AT, s, softplus_1e)
                    opening(b, "ln", ACT_AT, s, softplus_ln)
                    if scan:
                        for g in steps(ACT_AT, "z", s):
                            z_tanh(b, g)
                    if post:
                        for c in steps(ACT_AT, "x1t", s):
                            x1t_copy(b - 1, c)
                        for c in steps(ACT_AT, "gate", s):
                            gate_tanh(b - 1, c)
                    if scan:
                        for half in steps(ACT_AT, "fg", s):
                            fg_tanh(b, half)
                    if pre:
                        for j in steps(ACT_AT, "xi", s):
                            xi_copy(b + 1, j)
                        for j in steps(ACT_AT, "tanh", s):
                            xi_tanh(b + 1, j)
                        for part in steps(ACT_AT, "split", s):
                            split(b + 1, part)
                        for m in steps(ACT_AT, "bc", s):
                            bc_copy(b + 1, m)

            for dst, src in ((Eye3[:, :], eye3), (Dcol[:, :], d_skip), (Id[:, :], ident)):
                act.dma_start(dst, src).then_inc(w_const, 16)
            act.wait_ge(up_done, ONE)
            nc.scalar.activation(TanhC[:, 0:TB], Eps[:, 0, :], ACT.Tanh)
            act.wait_ge(conv_ready, 1)
            b = Batch(0)
            xi_copy(b, 0)
            for j in range(NK):
                if j + 1 < NK:
                    xi_copy(b, j + 1)
                xi_tanh(b, j)
            act.wait_ge(w_scan, 16 * LOADS["w_scan"])
            nc.scalar.activation(NegA[:, :, :], NegA[:, :, :], ACT.Exp).then_inc(a_exp, 1)
            split(b, 0)
            split(b, 1)
            softplus_abs(b, 0)
            softplus_e(b, 0)
            split(b, 2)
            softplus_1e(b, 0)
            softplus_abs(b, 1)
            softplus_e(b, 1)
            softplus_1e(b, 1)
            softplus_ln(b, 0)
            softplus_ln(b, 1)
            for n in range(ACT_AT["ahead"]):
                bc_copy(b, n)
            act.wait_ge(a_ready, 1)
            batches(act, iteration)

        @block.gpsimd
        def _(pool):
            def log1p(b, k):
                reach(pool, sp_ln, b, NK, k + 1)
                pool.wait_ge(sp_gain, b.times(NK, k + 1))
                nc.gpsimd.tensor_tensor(Sp_1e[:, k % 2, :], Sp_1e[:, k % 2, :], Sp_e[:, k % 2, :],
                                        ALU.subtract).then_inc(sp_sum, 1)

            def dt_u(b, k):
                reach(pool, dt_ready, b, NK, k + 1)
                reach(pool, u_ready, b, NK, NK)
                reach(pool, dBu_ready, b, UNITS, (k - 1) * NS)
                nc.gpsimd.tensor_tensor(DtU[:, k % 2, :], Dt[:, k, :], U[:, b.parity, k, :],
                                        ALU.mult).then_inc(dtu_ready, 1)

            def drive(b, k, n):
                unit = k * NS + n
                if k == 0:
                    reach(pool, B_ready, b, NS, n + 1)
                if n == 0:
                    pool.wait_ge(dtu_ready, b.times(NK, k + 1))
                reach(pool, h_ready, b, UNITS, unit + 1 - DBU_RING)
                nc.gpsimd.tensor_tensor(DBu[:, unit % DBU_RING, :], DtU[:, k % 2, :], Bc[:, n, :],
                                        ALU.mult).then_inc(dBu_ready, 1)

            def product(b, k, n):
                unit = k * NS + n
                reach(pool, h_ready, b, UNITS, unit + 1)
                if k == 0:
                    reach(pool, C_ready, b, NS, n + 1)
                nc.gpsimd.tensor_tensor(Prod[:, unit % PROD_RING, :], Prod[:, unit % PROD_RING, :], Cc[:, n, :],
                                        ALU.mult).then_inc(prod_pool, 1)

            def inverse_std(b, mv, Mv, var, Rs, rs, eps):
                reach(pool, mv, b, TB, TB)
                nc.gpsimd.tensor_tensor(Rs[:, :], Mv[:, :, 1], Eps[:, eps, :], ALU.add).then_inc(var, 1)
                pool.wait_ge(var, b.times(1, 1))
                nc.gpsimd.tensor_tensor(Rs[:, :], Rs[:, :], MinusHalf[:, :], ALU.pow).then_inc(rs, 1)

            def iteration(b):
                post, scan, pre = has_post(b), has_scan(b), has_pre(b)
                for s in range(UNITS):
                    k, n = divmod(s, NS)
                    if scan:
                        drive(b, k, n)
                        if s - POOL_LAG in POOL_UNITS:
                            product(b, *divmod(s - POOL_LAG, NS))
                    if first(b) and s == POOL_AT["log1"]:
                        log1p(b, 1)
                    opening(b, "log", POOL_AT, s, log1p)
                    opening(b, "dtu", POOL_AT, s, dt_u, early=1)
                    if post:
                        if s == POOL_AT["rs1"]:
                            inverse_std(b - 1, mv1, Mv1, var1, Rs1, rs1, 1)
                        if s == POOL_AT["rs2"]:
                            inverse_std(b - 1, mv2, Mv2, var2, Rs2, rs2, 0)

            pool.wait_ge(const_ready, 1)
            b = Batch(0)
            log1p(b, 0)
            dt_u(b, 0)
            batches(pool, iteration)

        @block.vector
        def _(dve):
            def tap(b, step):
                j, i = divmod(step, TAPS - 1)
                t = TAPS - 2 - i
                if i == 0:
                    reach(dve, xi_copied, b, NK, j + 1)
                reach(dve, tap_done, b, NK * (TAPS - 1), step)
                c = U[:, b.parity, j, :]
                nc.vector.scalar_tensor_tensor(c, xi_tile(b, j)[:, t:t + SEQ], ConvW[:, j, t:t + 1], c,
                                               ALU.mult, ALU.add).then_inc(tap_done, 1)

            def u(b, j):
                reach(dve, tanh_c, b, NK, j + 1)
                c = U[:, b.parity, j, :]
                nc.vector.scalar_tensor_tensor(c, tanh_tile(b, j), 1.0, c, ALU.add, ALU.mult).then_inc(u_ready, 1)

            def split_rest(b, part):
                if part == 0:
                    reach(dve, split_hi, b, 1, 1)
                    nc.vector.tensor_tensor(Dbl[0:BC_PARTS, :], W[BANK["x_proj"]][0:BC_PARTS, :], DblS[:, :],
                                            ALU.subtract).then_inc(rest1, 1)
                else:
                    reach(dve, split_mid, b, 1, 1)
                    nc.vector.tensor_tensor(Dbl[64:96, :], Dbl[64:96, :], DblS[64:96, :],
                                            ALU.subtract).then_inc(rest2, 1)

            def rounding(b, k):
                reach(dve, sp_1e, b, NK, k + 1)
                nc.vector.scalar_tensor_tensor(Sp_e[:, k % 2, :], Sp_1e[:, k % 2, :], -1.0, Sp_e[:, k % 2, :],
                                               ALU.add, ALU.subtract).then_inc(sp_gain, 1)

            def dt(b, k):
                reach(dve, sp_sum, b, NK, k + 1)
                nc.vector.tensor_tensor(Dt[:, k, :], Sp_1e[:, k % 2, :], Dt[:, k, :],
                                        ALU.add).then_inc(dt_ready, 1)

            def scan_unit(b, k, n):
                unit = k * NS + n
                reach(dve, dA_ready, b, UNITS, unit + 1)
                reach(dve, dBu_ready, b, UNITS, unit + 1)
                bank = dA[unit % DA_RING][:, :]
                h = bank
                if unit in POOL_UNITS:
                    reach(dve, y_added, b, UNITS, unit + 1 - PROD_RING)
                    h = Prod[:, unit % PROD_RING, :]
                nc.vector.tensor_tensor_scan(h, bank, DBu[:, unit % DBU_RING, :], 0.0,
                                             ALU.mult, ALU.add).then_inc(h_ready, 1)

            def product(b, k, n):
                unit = k * NS + n
                reach(dve, h_ready, b, UNITS, unit + 1)
                if k == 0:
                    reach(dve, C_ready, b, NS, n + 1)
                reach(dve, y_added, b, UNITS, unit + 1 - PROD_RING)
                nc.vector.tensor_tensor(Prod[:, unit % PROD_RING, :], dA[unit % DA_RING][:, :], Cc[:, n, :],
                                        ALU.mult).then_inc(prod_vec, 1)

            def z_silu(b, k):
                reach(dve, tanh_z, b, NK, k + 1)
                flat = G[:, :, :].rearrange("p t d -> p (t d)")
                nc.vector.scalar_tensor_tensor(flat, flat, 1.0, W[BANK["z"][k]][:, :], ALU.add, ALU.mult).then_inc(silu_z, 1)

            def gated(b, k):
                reach(dve, y_added, b, UNITS, (k + 1) * NS)
                dve.wait_ge(silu_z, b.times(NK, k + 1))
                flat = G[:, :, :].rearrange("p t d -> p (t d)")
                nc.vector.tensor_tensor(flat, Y[:, :], flat, ALU.mult).then_inc(g_ready, 1)

            def mix_term(b, step):
                half, term = divmod(step, 2)
                rows = slice(2 * half, 2 * half + 2)
                if term == 0:
                    if half == 0:
                        dve.wait_ge(xn_loaded, b.times(16, 16))
                    reach(dve, tanh_f, b, 2, half + 1)
                    nc.vector.scalar_tensor_tensor(X1[:, rows, :], TanhF[:, rows, :], 3.0, X1[:, rows, :],
                                                   ALU.add, ALU.mult).then_inc(mix_parts, 1)
                else:
                    reach(dve, nf_done, b, 2, half + 1)
                    dve.wait_ge(mix_parts, b.times(4, step))
                    nc.vector.scalar_tensor_tensor(TanhF[:, rows, :], TanhF[:, rows, :], -1.0,
                                                   W[BANK["nf"][half]][:, :].rearrange("p (t d) -> p t d", t=2),
                                                   ALU.add, ALU.mult).then_inc(mix_parts, 1)

            def mix(b, half):
                rows = slice(2 * half, 2 * half + 2)
                dve.wait_ge(mix_parts, b.times(4, 2 * half + 2))
                nc.vector.tensor_tensor(X1[:, rows, :], X1[:, rows, :], TanhF[:, rows, :],
                                        ALU.subtract).then_inc(mixed, 1)
                statistics(b, half, mixed, Stats1, stats1)

            def statistics(b, half, source, Stats, stats):
                dve.wait_ge(source, b.times(2, half + 1))
                for t in (2 * half, 2 * half + 1):
                    nc.vector.bn_stats(Stats[:, t, :], X1[:, t, :]).then_inc(stats, 1)

            def aggregate(Stats, Mv, mv, half):
                for t in (2 * half, 2 * half + 1):
                    nc.vector.bn_aggr(Mv[:, t, :], Stats[:, t, :]).then_inc(mv, 1)

            def normalize(b, rs, Mv, Rs, ready):
                reach(dve, rs, b, 1, 1)
                for t in range(TB):
                    ins = nc.vector.tensor_scalar(X1[:, t, :], X1[:, t, :], Mv[:, t, 0:1], Rs[:, t:t + 1],
                                                  ALU.subtract, ALU.mult)
                ins.then_inc(ready, 1)

            def gate_silu(b, c):
                reach(dve, tanh_g, b, NC, c + 1)
                nc.vector.scalar_tensor_tensor(Ht[:, c, :], Ht[:, c, :], 1.0, W[BANK["gate"][c]][:, :],
                                               ALU.add, ALU.mult).then_inc(silu_g, 1)

            def gate_up(b, c):
                reach(dve, up_done, b, NC, ONE + c + 1)
                dve.wait_ge(silu_g, b.times(NC, c + 1))
                nc.vector.tensor_tensor(Ht[:, c, :], W[BANK["up"][c]][:, :], Ht[:, c, :], ALU.mult).then_inc(hid_ready, 1)

            def residual(b, half):
                rows = slice(2 * half, 2 * half + 2)
                reach(dve, down_done, b, 2, ONE + half + 1)
                nc.vector.tensor_tensor(X1[:, rows, :], W[BANK["down"][half]][:, :].rearrange("p (t d) -> p t d", t=2),
                                        X1[:, rows, :], ALU.add).then_inc(summed, 1)
                statistics(b, half, summed, Stats2, stats2)

            def last_product(b):
                product(b, NK - 1, NS - 1)

            def iteration(b):
                post, scan, pre = has_post(b), has_scan(b), has_pre(b)
                for s in range(UNITS):
                    k, n = divmod(s, NS)
                    to_1 = [h for h in (0, 1) if post and s == DVE_AT["mix"][h] + 1]
                    to_2 = [h for h in (0, 1) if post and s == DVE_AT["sum"][h] + 1]
                    for h in to_1:
                        reach(dve, stats1, b - 1, TB, 2 * h + 2)
                    for h in to_2:
                        reach(dve, stats2, b - 1, TB, 2 * h + 2)
                    if first(b):
                        for i in steps(DVE_AT, "once", s):
                            once[i]()
                    if scan:
                        scan_unit(b, k, n)
                    for h in to_1:
                        aggregate(Stats1, Mv1, mv1, h)
                    for h in to_2:
                        aggregate(Stats2, Mv2, mv2, h)
                    if s == 0 and post:
                        last_product(b - 1)
                    if scan and s and s - 1 not in POOL_UNITS:
                        product(b, *divmod(s - 1, NS))
                    closing(b, "gated", DVE_AT, s, gated)
                    opening(b, "round", DVE_AT, s, rounding)
                    opening(b, "dt", DVE_AT, s, dt)
                    if scan:
                        for g in steps(DVE_AT, "z", s):
                            z_silu(b, g)
                    if pre:
                        for step in steps(DVE_AT, "taps", s):
                            tap(b + 1, step)
                        for j in steps(DVE_AT, "u", s):
                            u(b + 1, j)
                        for part in steps(DVE_AT, "split", s):
                            split_rest(b + 1, part)
                    if post:
                        for step in steps(DVE_AT, "terms", s):
                            mix_term(b - 1, step)
                        for half in steps(DVE_AT, "mix", s):
                            mix(b - 1, half)
                        if s == DVE_AT["x1"]:
                            normalize(b - 1, rs1, Mv1, Rs1, x1_ready)
                        for c in steps(DVE_AT, "gate", s):
                            gate_silu(b - 1, c)
                        for c in steps(DVE_AT, "up", s):
                            gate_up(b - 1, c)
                        for half in steps(DVE_AT, "sum", s):
                            residual(b - 1, half)
                        if s == DVE_AT["out"]:
                            normalize(b - 1, rs2, Mv2, Rs2, out_ready)

            def split_bias():
                rest, count = fgb_stage, 1
                for rows in (slice(0, 96), slice(32, 64), slice(64, 96), slice(64, 96)):
                    nc.vector.tensor_copy(FgS[rows, :], rest[rows, :]).then_inc(fgb_split, 1)
                    count += 1
                    dve.wait_ge(fgb_split, count)
                    if rows != slice(32, 64) and count < FGB_STEPS:
                        part = slice(0, 96) if rows == slice(0, 96) else slice(64, 96)
                        nc.vector.tensor_tensor(rest[part, :], rest[part, :], FgS[part, :],
                                                ALU.subtract).then_inc(fgb_split, 1)
                        count += 1
                        dve.wait_ge(fgb_split, count)
                assert count == FGB_STEPS

            def ffn_gate():
                dve.wait_ge(w_post, 16 * LOADS["w_post"])
                nc.vector.tensor_scalar(Wgate[:, :, :].rearrange("p k n -> p (k n)"), gate_stage, DEQUANT, None, ALU.mult)

            def ffn_up():
                nc.vector.tensor_scalar(Wup[:, :, :].rearrange("p k n -> p (k n)"), up_stage, DEQUANT, None, ALU.mult)

            def ffn_down():
                nc.vector.tensor_scalar(Wdown[:, :, :].rearrange("p k n -> p (k n)"), down_stage, DEQUANT, 0.5,
                                        ALU.mult, ALU.mult).then_inc(ffn_ready, 1)

            def bias():
                dve.wait_ge(fgb_loaded, 16 * 6)
                split_bias()

            def dt_1():
                dt(Batch(0), 1)

            once = (dt_1, ffn_gate, ffn_up, ffn_down, bias)

            nc.vector.memset(fgb_stage, 0.0).then_inc(fgb_split, 1)
            nc.vector.memset(Xi[:, 0:TAPS - 1], 0.0)
            nc.vector.memset(FirstXi[:, :, 0:TAPS - 1], 0.0)
            nc.vector.memset(Ones[:, :], 1.0).then_inc(stored, ONE)
            nc.vector.memset(MinusHalf[:, :], -0.5).then_inc(down_done, ONE)
            nc.vector.memset(Eps[:, 0, :], EPS).then_inc(gate_done, ONE)
            nc.vector.memset(Eps[:, 1, :], 4 * EPS).then_inc(up_done, ONE)
            nc.vector.memset(Dbl[DT_ROW:P, :], 1.0)
            dve.wait_ge(w_const, 16 * LOADS["w_const"])
            nc.vector.tensor_copy(Sel, Eye3[:, :].unsqueeze(2).broadcast_to([BC_PARTS, 2 * NS, P]))
            for k in range(NK):
                ins = nc.vector.tensor_scalar(DiagD[:, k, :], Id[:, :], Dcol[:, k:k + 1], None, ALU.mult)
            ins.then_inc(const_ready, 1)
            dve.wait_ge(w_in, 16 * LOADS["w_in"])
            nc.vector.tensor_scalar(ConvW[:, :, :], ConvW[:, :, :], 0.5, None, ALU.mult)
            nc.vector.tensor_scalar(ConvB[:, :], ConvB[:, :], 0.5, None, ALU.mult).then_inc(conv_ready, 1)
            dve.wait_ge(conv_ready, 1)
            b = Batch(0)
            for step in range(NK * (TAPS - 1)):
                tap(b, step)
                if step >= 5 and step % 3 == 2:
                    u(b, step // 3 - 1)
            u(b, NK - 1)
            dve.wait_ge(a_exp, 1)
            nc.vector.tensor_scalar(NegA[:, :, :], NegA[:, :, :], -1.0, None, ALU.mult).then_inc(a_ready, 1)
            split_rest(b, 0)
            split_rest(b, 1)
            rounding(b, 0)
            rounding(b, 1)
            dt(b, 0)
            batches(dve, iteration)


BANK = {
    "xi": "CBBA", "x_proj": "C", "v": "CCCC", "z": "ACAC", "fg": "BA", "gt": "CCBC", "nf": "CA", "x1t": "BC",
    "down": "CC", "gate": "AAACAA", "up": "BBBBBB",
}

PE_AT = {
    "open": (0, 16, 32, 50), "gt": (18, 32, 48, 1), "v": (42, 43, 13, 20), "z": (12, 23, 46, 58),
    "nf": (4, 4, 6, 9), "xi": (7, 10, 14, 20), "x1t": (16, 16), "gate": (22, 26, 31, 35, 38, 42),
    "up": (23, 30, 34, 36, 41, 42), "x_proj": 37, "fg": (46, 47), "down": (49, 50, 53, 54),
    "bc": (51, 52, 53, 54, 55, 56, 57, 59, 59, 60, 60, 62, 63, 64, 65, 66), "ahead": 8,
}
ACT_AT = {
    "gt": (22, 36, 52, 6), "ln": (52, 52, 27, 27), "z": (18, 33, 50, 63), "xi": (12, 15, 20, 24),
    "tanh": (14, 20, 24, 29), "x1t": (21, 21), "gate": (27, 32, 38, 39, 44, 46), "split": (42, 44, 47),
    "fg": (50, 52), "bc": (56, 57, 58, 59, 59, 60, 61, 63, 64, 65, 66, 67, 68, 69, 70, 71), "e": (45, 49, 21, 23),
    "abs": (45, 48, 21, 23), "ahead": 3, "1e": (46, 51, 22, 24),
}
DVE_AT = {
    "gated": (17, 33, 49, 2), "round": (48, 51, 22, 25), "dt": (54, 58, 27, 41), "z": (16, 32, 48, 62),
    "terms": (8, 9, 10, 12), "mix": (11, 14), "x1": 18, "taps": (12, 12, 12, 14, 15, 15, 21, 21, 21, 24, 24, 25),
    "u": (13, 23, 28, 29), "gate": (28, 32, 37, 39, 43, 47), "up": (30, 33, 38, 41, 43, 47), "split": (43, 45),
    "sum": (54, 58), "out": 60, "once": (6, 5, 5, 9, 12),
}
POOL_AT = {
    "log": (56, 58, 29, 40), "dtu": (57, 15, 31, 43), "rs1": 18, "rs2": 61, "log1": 1,
}


LOADS = {"w_in": 3, "w_const": 3, "w_scan": 8, "w_post": 5}
FGB_STEPS = 7


def steps(at, name, s):
    return [i for i, slot in enumerate(at[name]) if slot == s]


def pool_count(units):
    return sum(unit < units for unit in POOL_UNITS)


def vec_count(units):
    return units - pool_count(units)


def reach_product(eng, prod_vec, prod_pool, b, unit):
    if unit in POOL_UNITS:
        reach(eng, prod_pool, b, pool_count(UNITS), pool_count(unit) + 1)
    else:
        reach(eng, prod_vec, b, vec_count(UNITS), vec_count(unit) + 1)


def kernel(**inputs):
    import numpy as np
    import concourse.bacc as bacc
    from concourse.bass_utils import run_bass_kernel_spmd

    a = {n.replace("L0_attn_", "").replace("L0_ffn_", ""): np.asarray(v) for n, v in inputs.items()}
    eye = np.eye(P, dtype=np.float32)
    eye_bc = np.eye(2 * NS, dtype=np.float32)
    arrays = {
        "x": a["x"].reshape(BATCH * SEQ, DM),
        "xT": a["x"].transpose(0, 2, 1).reshape(BATCH * DM, SEQ),
        "in_w": a["in_proj_w"],
        "conv_w": a["conv_w"],
        "conv_b": a["conv_b"].reshape(NK, P).T,
        "xp_w": a["x_proj_w"],
        "dt_w": a["dt_proj_w"],
        "dt_b": a["dt_proj_b"],
        "a_log": a["A_log"],
        "d_skip": a["D"].reshape(NK, P).T,
        "out_w": a["out_proj_w"],
        "fg_w": a["fg_w"],
        "fg_b": a["fg_b"],
        "gate_wT": a["w_gate"].T,
        "up_wT": a["w_up"].T,
        "down_wT": a["w_down"].T,
        "ident": eye,
        "eye3": np.concatenate([eye_bc, eye_bc, eye_bc]),
    }
    nc = bacc.Bacc("TRN2", target_bir_lowering=False, num_devices=1)
    args = {}
    for name, v in arrays.items():
        arrays[name] = np.ascontiguousarray(v)
        args[name] = nc.dram_tensor(f"in_{name}", v.shape, mybir.dt.from_np(v.dtype), kind="ExternalInput").ap()
    out = nc.dram_tensor("out_dram", (BATCH * SEQ, DM), F32, kind="ExternalOutput").ap()
    build(nc, *args.values(), out)
    r = run_bass_kernel_spmd(nc, [{f"in_{n}": v for n, v in arrays.items()}], core_ids=[0])
    return r.results[0]["out_dram"].reshape(BATCH, SEQ, DM)
```
